# Optimizing a Trainium2 kernel written in Bass

```python
import numpy as np
import jax
import jax.numpy as jnp

def _softmax(x, axis=-1):
    return jax.nn.softmax(x, axis=axis)

def _gelu(x):
    return jax.nn.gelu(x, approximate=True)

def _silu(x):
    return jax.nn.silu(x)

def _sigmoid(x):
    return jax.nn.sigmoid(x)

def _layernorm(x, axis=-1, eps=1e-05):
    m = jnp.mean(x, axis=axis, keepdims=True)
    v = jnp.var(x, axis=axis, keepdims=True)
    return (x - m) / jnp.sqrt(v + eps)

def _scatter_add(tgt, idx, src, axis=0):
    return tgt.at[idx].add(src)

def _segment_sum(src, seg, n):
    return jax.ops.segment_sum(src, seg, n)
kernel_name = 'mk_adj_resnorm_d2_adj_r2_a0db2c'

def setup_inputs(seed: int=0):
    np.random.seed(seed)
    _w = jnp.asarray

    def _rec_inputs():
        import jax
        import jax.numpy as jnp
        _gk = jax.random.key(seed)
        x = 7.22e-05 + 1 * jax.random.normal(jax.random.fold_in(_gk, 1), (2048, 512), jnp.float32)
        _w = (1.0 + jnp.arange(2048, dtype=jnp.float32)) ** (-0.5)
        _w = _w / _w.mean()
        _pij = jnp.clip(0.00195312 * _w[:, None] * _w[None, :], 0.0, 1.0)
        _a = jax.random.uniform(jax.random.fold_in(_gk, 2), (2048, 2048)) < _pij
        _a = jnp.logical_or(_a, jnp.swapaxes(_a, -1, -2))
        _a = jnp.logical_or(_a, jnp.eye(2048, dtype=bool))
        _af = _a.astype(jnp.float32)
        _d = jnp.maximum(_af.sum(-1), 1.0) ** (-0.5)
        _af = _af * _d[..., :, None] * _d[..., None, :]
        adj = _af
        return (x, adj)
    x, adj = _rec_inputs()

    def _L0_gnn_setup():
        import jax, jax.numpy as jnp
        import numpy as np
        N = 4096
        D = 512

        def adjacent_mat(adj):
            adj = adj + jnp.eye(adj.shape[0], dtype=adj.dtype)
            deg = jnp.sum(adj, axis=1)
            dinv = jnp.where(deg > 0, deg ** (-0.5), 0.0).astype(adj.dtype)
            return dinv[:, None] * adj * dinv[None, :]
        key = jax.random.key(seed)
        k1, k2 = jax.random.split(key)
        x = jax.random.normal(k1, (N, D), dtype=jnp.float32)
        Coefficient2 = 1e-08 * jnp.ones((N, N), dtype=jnp.float32)
        A = jax.random.uniform(k2, (N, N), dtype=jnp.float32)
        return {'x': x, 'Coefficient2': Coefficient2, 'A': A}
    _L0_gnn_all = _L0_gnn_setup()
    _L0_gnn_in = {k: v for k, v in _L0_gnn_all.items() if k in ()}
    del _L0_gnn_all

    def _L1_gnn_setup():
        import jax, jax.numpy as jnp
        import numpy as np
        N = 2048
        D_IN = 512
        H = 16
        DH = D_IN // H
        ALPHA = 0.2
        MASK_VAL = -65500.0
        key = jax.random.key(seed)
        ks = jax.random.split(key, 7)
        x = jax.random.normal(ks[0], (N, D_IN), dtype=jnp.float32)
        adj = jax.random.randint(ks[1], (N, N), 0, 2).astype(jnp.float32)
        s = 1.0 / np.sqrt(D_IN)
        W_seq = jax.random.normal(ks[2], (D_IN, D_IN), dtype=jnp.float32) * s
        a1 = jax.random.normal(ks[3], (DH,), dtype=jnp.float32) / np.sqrt(DH)
        a2 = jax.random.normal(ks[4], (DH,), dtype=jnp.float32) / np.sqrt(DH)
        W_out = jax.random.normal(ks[5], (D_IN, D_IN), dtype=jnp.float32) * s
        b_out = jax.random.normal(ks[6], (D_IN,), dtype=jnp.float32) * 0.01
        return {'x': x, 'adj': adj, 'W_seq': W_seq, 'a1': a1, 'a2': a2, 'W_out': W_out, 'b_out': b_out}
    _L1_gnn_all = _L1_gnn_setup()
    _L1_gnn_in = {k: v for k, v in _L1_gnn_all.items() if k in ('W_seq', 'a1', 'a2', 'W_out', 'b_out')}
    del _L1_gnn_all
    return {'x': x, 'adj': adj, 'L1_gnn_W_seq': _L1_gnn_in['W_seq'], 'L1_gnn_a1': _L1_gnn_in['a1'], 'L1_gnn_a2': _L1_gnn_in['a2'], 'L1_gnn_W_out': _L1_gnn_in['W_out'], 'L1_gnn_b_out': _L1_gnn_in['b_out']}

def reference(x, adj, L1_gnn_W_seq, L1_gnn_a1, L1_gnn_a2, L1_gnn_W_out, L1_gnn_b_out):
    import jax
    import jax.numpy as jnp

    def _L0_gnn_ref(x, Coefficient2, A):
        import jax, jax.numpy as jnp
        import numpy as np
        N = 4096
        D = 512

        def adjacent_mat(adj):
            adj = adj + jnp.eye(adj.shape[0], dtype=adj.dtype)
            deg = jnp.sum(adj, axis=1)
            dinv = jnp.where(deg > 0, deg ** (-0.5), 0.0).astype(adj.dtype)
            return dinv[:, None] * adj * dinv[None, :]
        A_c = jax.lax.stop_gradient(A)
        adj = adjacent_mat((A_c + A_c.T) * 0.5)
        y = Coefficient2 @ adj
        y = y @ x
        return y

    def _L1_gnn_ref(x, adj, W_seq, a1, a2, W_out, b_out):
        import jax, jax.numpy as jnp
        import numpy as np
        N = 2048
        D_IN = 512
        H = 16
        DH = D_IN // H
        ALPHA = 0.2
        MASK_VAL = -65500.0
        seq = (x @ W_seq).reshape(N, H, DH)
        score1 = jnp.einsum('nhd,d->hn', seq, a1)
        score2 = jnp.einsum('nhd,d->hn', seq, a2)
        scores = score1[:, :, None] + score2[:, None, :]
        scores = jax.nn.leaky_relu(scores, negative_slope=ALPHA)
        scores = scores + (1.0 - adj)[None, :, :] * MASK_VAL
        attn = jax.nn.softmax(scores, axis=-1)
        hidden = jnp.einsum('hij,jhd->ihd', attn, seq).reshape(N, D_IN)
        hidden = hidden @ W_out + b_out
        return jax.nn.elu(hidden)
    x = _layernorm(x + _L0_gnn_ref(x, adj, adj), axis=-1)
    x = _layernorm(x + _L1_gnn_ref(x, adj, L1_gnn_W_seq, L1_gnn_a1, L1_gnn_a2, L1_gnn_W_out, L1_gnn_b_out), axis=-1)
    return x

_drawn_inputs = setup_inputs


def setup_inputs(seed=0):
    import zlib

    import numpy as np

    out = dict(_drawn_inputs(seed))
    spreads = {}
    factors = {'L1_gnn_b_out': 8.0}
    for name, (base, spread) in spreads.items():
        noise = np.random.default_rng([zlib.crc32(name.encode()), seed]).standard_normal(out[name].shape)
        drawn = base * np.exp(spread * noise) if base else spread * noise
        out[name] = jnp.asarray(drawn.astype(out[name].dtype))
    for name, factor in factors.items():
        out[name] = (out[name] * factor).astype(out[name].dtype)
    return out
```

```python
import concourse.bass as bass
from concourse import mybir
from contextlib import ExitStack

F32 = mybir.dt.float32
F32R = mybir.dt.float32r
I32 = mybir.dt.int32
U32 = mybir.dt.uint32
ALU = mybir.AluOpType
ACT = mybir.ActivationFunctionType
AX = mybir.AxisListType
RMAX = bass.bass_isa.ReduceOp.max

P = 128
N = 2048
D = 512
NB = N // P
CT = D // P
H = 16
DH = D // H
ROW = D + H
TOP = 8
SLOTS = TOP - 1
NARROW = 4
ALPHA = 0.2
MASK = -65500.0
FAR = 110.0
EPS = 1e-5


def pairs(eng, body):
    body(0, 0)
    body(1, 1)
    with eng.Fori(1, NB // 2 - 1) as g:
        body(g * 2, 0)
        body(g * 2 + 1, 1)
    body(NB - 2, 0)
    body(NB - 1, 1)


def exists(b):
    return not isinstance(b, int) or 0 <= b < NB


class Chain:

    def __init__(self, eng, sem, done):
        self.eng, self.sem, self.done = eng, sem, done

    def __call__(self, step):
        step.then_inc(self.sem, 1)
        self.done = self.done + 1
        self.eng.wait_ge(self.sem, self.done)



def graph_kernel(nc, x, adj, w_seq, a1, a2, w_out, b_out, out):
    with ExitStack() as ctx:
        base = nc.sbuf_base + (-nc.sbuf_base) % 64
        K = 1024

        def at(name, offset, shape, dtype=F32):
            return nc.alloc_sbuf_tensor_at(name, shape, dtype, offset=base + offset)

        def psum(name, shape):
            return ctx.enter_context(nc.psum_tensor(name, shape, F32))

        def sem(name):
            return ctx.enter_context(nc.semaphore(name))

        v_hi = at("v_hi", 0, [P, NB, D], F32R)
        v_lo = at("v_lo", 32 * K, [P, NB, D], F32R)
        w_part = [at("w_hi", 0, [P, CT, D], F32R), at("w_lo", 8 * K, [P, CT, D], F32R)]
        wo_part = [at("wo_hi", 16 * K, [P, CT, D], F32R), at("wo_lo", 24 * K, [P, CT, D], F32R)]
        x1 = at("x1", 32 * K, [P, NB, D])
        w_raw = at("w_raw", 48 * K, [P, CT, D])
        wo_raw = at("wo_raw", 56 * K, [P, CT, D])
        xs = at("xs", 64 * K, [P, NB, D])
        z_hi = at("z_hi", 64 * K, [P, NB, D], F32R)
        z_lo = at("z_lo", 96 * K, [P, NB, D], F32R)
        rows_got = [at(f"rows_got{u}", 64 * K + u * 15 * K, [P, SLOTS, ROW]) for u in range(2)]
        rows_weighted = [at(f"rows_weighted{u}", 96 * K + u * 15 * K, [P, SLOTS, D]) for u in range(2)]
        hidden = at("hidden", 64 * K, [P, NB, D])
        stage = [at(f"stage{q}", (128 + 8 * q) * K, [P, N]) for q in range(4)]
        small = 144 * K
        a1b = at("a1b", small, [P, D])
        a2b = at("a2b", small + 2 * K, [P, D])
        bob = at("bob", small + 4 * K, [P, D])
        score_products = [at(f"score_products{i}", small + (6 + 2 * i) * K, [P, D]) for i in range(2)]
        table_tile = [at(f"table_tile{u}", small + 10 * K + u * 2112, [P, ROW]) for u in range(2)]
        top_val = at("top_val", small + 10 * K + 4224, [P, NB, TOP])
        top_idx = at("top_idx", small + 10 * K + 4736, [P, NB, TOP], U32)
        gather_idx = [at(f"gather_idx{u}", small + 10 * K + 5248 + 32 * u, [P, TOP], U32) for u in range(2)]
        scores = [at(f"scores{i}", small + 6 * K + i * 512, [P, SLOTS, H]) for i in range(3)]
        far_mask = at("far_mask", small + 8 * K, [P, NB, TOP])
        idx_f = at("idx_f", small + 8 * K + 512, [P, NB, TOP])
        slot_idx = at("slot_idx", small + 9 * K, [P, NB, TOP], U32)
        m_hi = [at(f"m_hi{u}", (160 + 16 * u) * K, [P, NB, P], F32R) for u in range(2)]
        m_lo = [at(f"m_lo{u}", (168 + 16 * u) * K, [P, NB, P], F32R) for u in range(2)]
        dense_s2 = at("dense_s2", 160 * K, [P, N])
        dense_score = at("dense_score", 168 * K, [P, N])
        dense_tmp = at("dense_tmp", 176 * K, [P, N])
        dense_pT = at("dense_pT", 184 * K, [P, NB, P])
        dense_seq = at("dense_seq", 136 * K, [P, NB, DH])
        x_tile = [at(f"x_tile{u}", (192 + 2 * u) * K, [P, D]) for u in range(2)]
        x_norm = [at(f"x_norm{u}", (196 + 2 * u) * K, [P, D]) for u in range(2)]
        t_hi = at("t_hi", 200 * K, [P, CT, P], F32R)
        t_lo = at("t_lo", 202 * K, [P, CT, P], F32R)
        ident = at("ident", 204 * K, [P, P])
        s1 = at("s1", 204 * K + 512, [P, NB, H])
        tail = [205 * K + 512]

        def little(name, shape, dtype=F32):
            size = 4
            for s in shape[1:]:
                size *= s
            tail[0] += size + -size % 32
            return at(name, tail[0] - size - -size % 32, shape, dtype)

        ones = little("ones", [P, 1])
        row_sum = little("row_sum", [P, NB])
        deg = little("deg", [P, NB])
        deg_pos = little("deg_pos", [P, NB])
        neg_half = little("neg_half", [P, NB])
        deg_pow = little("deg_pow", [P, NB])
        dinv = little("dinv", [P, NB])
        stats = little("stats", [P, 6])
        mean_var = little("mean_var", [P, 2])
        var_eps = little("var_eps", [P, 1])
        rstd = little("rstd", [P, 1])
        s2_range = little("s2_range", [P, 2 * H])
        s2_all = little("s2_all", [P, 2 * H])
        far = little("far", [P, 2])
        needs = little("needs", [P, 1 + NB])
        needs_all = little("needs_all", [P, 1 + NB])
        flags = little("flags", [P, 1 + NB], I32)
        block_val = little("block_val", [P, TOP])
        block_idx = little("block_idx", [P, TOP], U32)
        smax = little("smax", [P, H])
        ssum = little("ssum", [P, H])
        col = little("col", [P, 4])

        ps_t = psum("ps_t", [P, NB, P])
        ps_y = psum("ps_y", [P, 2, D])
        ps_x = psum("ps_x", [P, CT, P])
        ps_q = psum("ps_q", [P, D])

        table = nc.dram_tensor("table", [N, ROW], F32).ap()
        s2_rows = nc.dram_tensor("s2_rows", [H, N], F32).ap()

        x_b = x.rearrange("(b p) d -> b p d", p=P)
        out_b = out.rearrange("(b p) d -> b p d", p=P)
        adj_b = adj.rearrange("(b p) j -> b p j", p=P)
        adj_c = adj.rearrange("(k p) (b i) -> b p k i", p=P, i=P)
        table_b = table.rearrange("(b p) d -> b p d", p=P)
        w_v = w_seq.rearrange("(c p) d -> p c d", p=P)
        wo_v = w_out.rearrange("(c p) d -> p c d", p=P)

        def row_of(v):
            return v.rearrange("(a d) -> a d", a=1).to_broadcast([P, v.shape[0]])

        x_in = sem("x_in")
        first_in = [sem(f"first_in{q}") for q in range(4)]
        consts = sem("consts")
        col_summed = sem("col_summed")
        row_summed = sem("row_summed")
        deg_step = sem("deg_step")
        deg_ready = sem("deg_ready")
        pow_ready = sem("pow_ready")
        dinv_ready = sem("dinv_ready")
        vhi_ready = sem("vhi_ready")
        v_ready = sem("v_ready")
        rows_in = [sem(f"rows_in{u}") for u in range(2)]
        cols_in = [sem(f"cols_in{u}") for u in range(2)]
        turned = sem("turned")
        s_summed = sem("s_summed")
        t_read = sem("t_read")
        hi_ready = sem("hi_ready")
        lo_ready = sem("lo_ready")
        prod1_done = sem("prod1_done")
        zt_step = sem("zt_step")
        zt_ready = sem("zt_ready")
        zhi_ready = sem("zhi_ready")
        z_ready = sem("z_ready")
        small_in = sem("small_in")
        w_in = sem("w_in")
        whi_ready = sem("whi_ready")
        w_ready = sem("w_ready")
        xt_in = [sem(f"xt_in{u}") for u in range(2)]
        prod2_done = sem("prod2_done")
        y_read = sem("y_read")
        norm_step = sem("norm_step")
        var_ready = sem("var_ready")
        rstd_ready = sem("rstd_ready")
        x1_ready = sem("x1_ready")
        x1_kept = sem("x1_kept")
        x1_turned = sem("x1_turned")
        thi_ready = sem("thi_ready")
        t_ready = sem("t_ready")
        seq_done = sem("seq_done")
        seq_copied = sem("seq_copied")
        products_ready = sem("products_ready")
        tab_step = sem("tab_step")
        tab_ready = sem("tab_ready")
        tab_out = [sem(f"tab_out{u}") for u in range(2)]
        top_step = sem("top_step")
        top_done = sem("top_done")
        top_kept = sem("top_kept")
        range_ready = sem("range_ready")
        range_all = sem("range_all")
        far_step = sem("far_step")
        needs_ready = sem("needs_ready")
        needs_reduced = sem("needs_reduced")
        flags_ready = sem("flags_ready")
        table_done = sem("table_done")
        got_clear = sem("got_clear")
        passed = sem("passed")

        class Path:

            def __init__(self, name):
                self.idx_ready = sem(name + "idx_ready")
                self.got = [sem(name + f"got{u}") for u in range(2)]
                self.weigh_step = sem(name + "weigh_step")
                self.shifted = sem(name + "shifted")
                self.exp_ready = sem(name + "exp_ready")
                self.weighted = sem(name + "weighted")
                self.turned = sem(name + "turned")
                self.hi_ready = sem(name + "hi_ready")
                self.lo_ready = sem(name + "lo_ready")
                self.projected = sem(name + "projected")
                self.tail_step = sem(name + "tail_step")
                self.min_ready = sem(name + "min_ready")
                self.elu_exp = sem(name + "elu_exp")
                self.var_ready = sem(name + "var_ready")
                self.rstd_ready = sem(name + "rstd_ready")
                self.out_ready = sem(name + "out_ready")
                self.out_done = [sem(name + f"out_done{u}") for u in range(2)]

        near = Path("near_")
        full = Path("full_")
        s2_turned = sem("s2_turned")
        head_in = sem("head_in")
        block_in = sem("block_in")
        dense_step = sem("dense_step")
        dense_shifted = sem("dense_shifted")
        dense_exp = sem("dense_exp")
        dense_turned = sem("dense_turned")
        dense_copied = sem("dense_copied")
        dense_prod = sem("dense_prod")
        dense_block = sem("dense_block")

        def apart(eng):
            eng.sem_inc(passed, 1)

        block = ctx.enter_context(nc.Block())

        @block.sync
        def _(sp):
            for q in range(4):
                sp.dma_start(stage[q][:], adj_b[q]).then_inc(first_in[q], 16)
            with sp.Fori(1, NB // 4) as g:
                for q in range(4):
                    sp.wait_ge(col_summed, g * 4 + (q - 3))
                    sp.wait_ge(row_summed, g * 4 + (q - 3))
                    sp.dma_start(stage[q][:], adj_b[g * 4 + q]).then_inc(first_in[q], 16)
            sp.wait_ge(col_summed, NB)
            sp.wait_ge(row_summed, NB)

            def load_rows(n, b, u):
                sp.dma_start(stage[u][:], adj_b[b]).then_inc(rows_in[u], 16)

            def load_cols(b, u):
                sp.dma_start(stage[2 + u][:].rearrange("p (k i) -> p k i", i=P), adj_c[b]).then_inc(cols_in[u], 16)

            for u in range(2):
                load_rows(u, u, u)
                load_cols(u, u)

            def first(b, u):
                sp.wait_ge(turned, b + 1)
                apart(sp)
                if isinstance(b, int) and b + 2 >= NB:
                    load_rows(b + 2, b + 2 - NB, u)
                else:
                    load_rows(b + 2, b + 2, u)
                    sp.wait_ge(lo_ready, b + 1)
                    load_cols(b + 2, u)
            pairs(sp, first)

            sp.wait_ge(z_ready, NB)
            sp.dma_start(w_raw[:], w_v).then_inc(w_in, 16)
            sp.dma_start(wo_raw[:], wo_v).then_inc(w_in, 16)
            for vec, tile in ((a1, a1b), (a2, a2b)):
                for h in range(H):
                    sp.dma_start(tile[:, h * DH:(h + 1) * DH], row_of(vec)).then_inc(small_in, 16)
            sp.dma_start(bob[:], row_of(b_out)).then_inc(small_in, 16)
            for u in range(2):
                sp.dma_start(x_tile[u][:], x_b[u]).then_inc(xt_in[u], 16)

            def store_table(b, u):
                sp.wait_ge(tab_ready, b + 1)
                sp.dma_start(table_b[b], table_tile[u][:]).then_inc(tab_out[u], 16)

            def second(b, u):
                if not isinstance(b, int) or b + 2 < NB:
                    sp.wait_ge(turned, b + (NB + 1))
                    apart(sp)
                    sp.wait_ge(top_done, b + 1)
                    load_rows(b + 2 + NB, b + 2, u)
                if not isinstance(b, int) or 1 <= b < NB - 1:
                    sp.wait_ge(x1_ready, b)
                    sp.dma_start(x_tile[1 - u][:], x_b[b + 1]).then_inc(xt_in[1 - u], 16)
                if exists(b - 1):
                    store_table(b - 1, 1 - u)
            pairs(sp, second)
            store_table(NB - 1, 1)
            for u in range(2):
                sp.wait_ge(tab_out[u], 16 * NB // 2)
            sp.sem_inc(table_done, 1)

            def store_out(path):
                def store(b, u):
                    sp.wait_ge(path.out_ready, b + 1)
                    sp.dma_start(out_b[b], x_norm[u][:]).then_inc(path.out_done[u], 16)
                pairs(sp, store)
                for u in range(2):
                    sp.wait_ge(path.out_done[u], 16 * NB // 2)

            sp.wait_ge(flags_ready, 1)
            dense = sp.value_load(flags[0:1, 0:1], min_val=0, max_val=1)
            with sp.If(dense == 0):
                store_out(near)
            with sp.Else():
                with nc.allow_non_contiguous_dma(reason="neighbour scores by head, once"):
                    sp.dma_start(s2_rows.rearrange("h (j o) -> h j o", o=1),
                                 table[:, D:ROW].rearrange("j (h o) -> h j o", o=1)).then_inc(s2_turned, 16)
                sp.wait_ge(s2_turned, 16)
                with sp.Fori(0, H) as h:
                    sp.wait_ge(dense_block, h * NB + 1)
                    sp.dma_start(dense_s2[:], row_of(s2_rows[h])).then_inc(head_in, 16)
                    sp.dma_start(dense_seq[:], table[:, bass.ds(h * DH, DH)].rearrange("(k p) d -> p k d", p=P)).then_inc(head_in, 16)
                    with sp.Fori(0, NB) as b:
                        sp.wait_ge(dense_block, h * NB + b + 1)
                        sp.dma_start(stage[0][:], adj_b[b]).then_inc(block_in, 16)
                store_out(full)
            sp.nop()

        @block.gpsimd
        def _(pool):
            nc.gpsimd.memset(ident[:], 0.0).then_inc(consts, 1)
            nc.gpsimd.memset(neg_half[:], -0.5)
            nc.gpsimd.memset(ones[:], 1.0).then_inc(consts, 1)
            pool.wait_ge(consts, 2)
            nc.gpsimd.affine_select(out=ident[:], in_=ident[:], compare_op=ALU.not_equal, fill=1.0, base=0,
                                    pattern=[[-1, P]], channel_multiplier=1).then_inc(consts, 1)
            pool.wait_ge(deg_ready, 1)
            nc.gpsimd.tensor_tensor(deg_pow[:], deg_pos[:], neg_half[:], ALU.pow).then_inc(pow_ready, 1)

            def inv_std(ready, done, b):
                pool.wait_ge(ready, b + 1)
                nc.gpsimd.tensor_tensor(rstd[:], var_eps[:], neg_half[:, 0:1], ALU.pow).then_inc(done, 1)

            def second(b, u):
                if exists(b - 1):
                    inv_std(var_ready, rstd_ready, b - 1)
                    products(b - 1, 1 - u)

            def products(b, u):
                pool.wait_ge(seq_copied, b + 1)
                if exists(b - 1):
                    pool.wait_ge(tab_ready, b)
                else:
                    pool.wait_ge(small_in, 16 * (2 * H + 1))
                nc.gpsimd.tensor_tensor(score_products[0][:], table_tile[u][:, 0:D], a1b[:], ALU.mult).then_inc(products_ready, 1)
                nc.gpsimd.tensor_tensor(score_products[1][:], table_tile[u][:, 0:D], a2b[:], ALU.mult).then_inc(products_ready, 1)
            pairs(pool, second)
            inv_std(var_ready, rstd_ready, NB - 1)
            products(NB - 1, 1)

            pool.wait_ge(prod2_done, NB)
            for u in range(2):
                nc.gpsimd.memset(rows_got[u][:], 0.0).then_inc(got_clear, 1)
            pool.wait_ge(range_ready, 1)
            nc.gpsimd.partition_all_reduce(s2_all[:], s2_range[:], P, RMAX).then_inc(range_all, 1)
            pool.wait_ge(needs_ready, 1)
            nc.gpsimd.partition_all_reduce(needs_all[:], needs[:], P, RMAX).then_inc(needs_reduced, 1)

            pool.wait_ge(flags_ready, 1)
            pool.wait_ge(table_done, 1)
            dense = pool.value_load(flags[0:1, 0:1], min_val=0, max_val=1)
            with pool.If(dense == 0):
                def gather(b, u):
                    pool.wait_ge(near.idx_ready, b + 1)
                    apart(pool)
                    for k in range(SLOTS):
                        nc.gpsimd.indirect_dma_start(
                            out=rows_got[u][:, k, :], out_offset=None, in_=table,
                            in_offset=bass.IndirectOffsetOnAxis(ap=gather_idx[u][:, k:k + 1], axis=0),
                            bounds_check=N - 1, oob_is_err=False).then_inc(near.got[u], 16)

                def step(b, u):
                    if exists(b + 1):
                        gather(b + 1, 1 - u)
                    if exists(b - 2):
                        inv_std(near.var_ready, near.rstd_ready, b - 2)
                pool.wait_ge(got_clear, 2)
                gather(0, 0)
                pairs(pool, step)
                inv_std(near.var_ready, near.rstd_ready, NB - 2)
                inv_std(near.var_ready, near.rstd_ready, NB - 1)
            with pool.Else():
                def step(b, u):
                    if exists(b - 1):
                        inv_std(full.var_ready, full.rstd_ready, b - 1)
                pairs(pool, step)
                inv_std(full.var_ready, full.rstd_ready, NB - 1)
            pool.nop()

        @block.scalar
        def _(act):
            act.dma_start(xs[:], x.rearrange("(b p) d -> p b d", p=P)).then_inc(x_in, 16)
            act.wait_ge(x_in, 16)
            act.wait_ge(dinv_ready, 1)
            with act.Fori(0, NB) as k:
                nc.scalar.activation(v_hi[:, k, :], xs[:, k, :], ACT.Copy, scale=dinv[:, bass.ds(k, 1)]).then_inc(vhi_ready, 1)

            def lead_s(b, u):
                act.wait_ge(s_summed, b + 1)
                if exists(b - 2):
                    act.wait_ge(prod1_done, b - 1)
                nc.scalar.copy(m_hi[u][:], stage[2 + u][:].rearrange("p (k i) -> p k i", i=P)).then_inc(hi_ready, 1)

            def lead_a(b, u):
                act.wait_ge(turned, b + (NB + 1))
                if exists(b - 2):
                    act.wait_ge(prod2_done, b - 1)
                else:
                    act.wait_ge(prod1_done, NB - 1 + b)
                nc.scalar.copy(m_hi[u][:], ps_t[:]).then_inc(hi_ready, 1)

            def lead_z(b, u):
                act.wait_ge(zt_ready, b + 1)
                nc.scalar.activation(z_hi[:, b, :], x_norm[u][:], ACT.Copy, scale=dinv[:, bass.ds(b, 1)]).then_inc(zhi_ready, 1)

            lead_s(0, 0)

            def first(b, u):
                if exists(b + 1):
                    lead_s(b + 1, 1 - u)
                else:
                    lead_a(0, 0)
                if exists(b - 1):
                    lead_z(b - 1, 1 - u)
            pairs(act, first)
            lead_z(NB - 1, 1)

            act.wait_ge(w_in, 32)
            nc.scalar.copy(w_part[0][:], w_raw[:]).then_inc(whi_ready, 1)
            nc.scalar.copy(wo_part[0][:], wo_raw[:]).then_inc(whi_ready, 1)

            def keep(b, u):
                act.wait_ge(x1_turned, b + 1)
                if exists(b - 1):
                    act.wait_ge(seq_done, b)
                nc.scalar.copy(t_hi[:], ps_x[:]).then_inc(thi_ready, 1)
                if not exists(b - 1):
                    act.wait_ge(w_ready, 2)
                nc.scalar.copy(x1[:, b, :], x_norm[u][:]).then_inc(x1_kept, 1)
                act.wait_ge(seq_done, b + 1)
                if exists(b - 2):
                    act.wait_ge(tab_out[u], b * 8 if u == 0 else b * 8 - 8)
                nc.scalar.copy(table_tile[u][:, 0:D], ps_q[:]).then_inc(seq_copied, 1)

            def second(b, u):
                if exists(b + 1):
                    lead_a(b + 1, 1 - u)
                if exists(b - 1):
                    keep(b - 1, 1 - u)
            pairs(act, second)
            keep(NB - 1, 1)

            def lead_hidden(path, b):
                act.wait_ge(path.turned, b + 1)
                if exists(b - 1):
                    act.wait_ge(path.projected, b)
                nc.scalar.copy(t_hi[:], ps_x[:]).then_inc(path.hi_ready, 1)

            def elu_exp(path, b, u):
                act.wait_ge(path.min_ready, b + 1)
                nc.scalar.activation(x_norm[u][:], x_norm[u][:], ACT.Exp).then_inc(path.elu_exp, 1)

            act.wait_ge(flags_ready, 1)
            dense = act.value_load(flags[0:1, 0:1], min_val=0, max_val=1)
            with act.If(dense == 0):
                def exp_slots(b):
                    act.wait_ge(near.shifted, b + 1)
                    nc.scalar.activation(scores[1][:], scores[0][:], ACT.Exp).then_inc(near.exp_ready, 1)

                def step(b, u):
                    exp_slots(b)
                    if exists(b - 1):
                        lead_hidden(near, b - 1)
                    if exists(b - 2):
                        elu_exp(near, b - 2, u)
                pairs(act, step)
                lead_hidden(near, NB - 1)
                elu_exp(near, NB - 2, 0)
                elu_exp(near, NB - 1, 1)
            with act.Else():
                with act.Fori(0, H * NB) as t:
                    act.wait_ge(dense_shifted, t + 1)
                    nc.scalar.activation(dense_tmp[:], dense_score[:], ACT.Exp, bias=col[:, 1:2],
                                         accum_out=col[:, 2:3]).then_inc(dense_exp, 1)
                    act.wait_ge(dense_turned, t + 1)
                    nc.scalar.copy(dense_pT[:], ps_t[:]).then_inc(dense_copied, 1)

                def step(b, u):
                    lead_hidden(full, b)
                    if exists(b - 1):
                        elu_exp(full, b - 1, 1 - u)
                pairs(act, step)
                elu_exp(full, NB - 1, 1)
            act.nop()

        @block.vector
        def _(dve):
            def first_sum(b, q):
                nc.vector.reduce_sum(row_sum[:, bass.ds(b, 1)], stage[q][:], AX.X).then_inc(row_summed, 1)

            with dve.Fori(0, NB // 4) as g:
                for q in range(4):
                    dve.wait_ge(first_in[q], g * 16 + 16)
                    first_sum(g * 4 + q, q)
            dve.wait_ge(row_summed, NB)
            dve.wait_ge(col_summed, NB)
            step = Chain(dve, deg_step, 0)
            step(nc.vector.tensor_tensor(deg[:], ps_q[:, 0:NB], row_sum[:], ALU.add))
            step(nc.vector.tensor_scalar(deg[:], deg[:], 0.5, 1.0, ALU.mult, ALU.add))
            nc.vector.tensor_scalar(deg_pos[:], deg[:], 1.2e-38, None, ALU.max).then_inc(deg_ready, 1)
            dve.wait_ge(pow_ready, 1)
            nc.vector.scalar_tensor_tensor(out=dinv[:], in0=deg[:], scalar=0.0, in1=deg_pow[:],
                                           op0=ALU.is_gt, op1=ALU.mult).then_inc(dinv_ready, 1)
            dve.wait_ge(dinv_ready, 1)
            with dve.Fori(0, NB) as k:
                dve.wait_ge(vhi_ready, k + 1)
                nc.vector.scalar_tensor_tensor(out=v_lo[:, k, :], in0=xs[:, k, :], scalar=dinv[:, bass.ds(k, 1)],
                                               in1=v_hi[:, k, :].bitcast(F32), op0=ALU.mult, op1=ALU.subtract).then_inc(v_ready, 1)

            def cols(u):
                return stage[2 + u][:].rearrange("p (k i) -> p k i", i=P)

            def sum_s(b, u):
                dve.wait_ge(turned, b + 1)
                dve.wait_ge(cols_in[u], b * 8 + 16 - 8 * u)
                nc.vector.tensor_tensor(cols(u), ps_t[:], cols(u), ALU.add).then_inc(s_summed, 1)

            def rest_s(b, u):
                dve.wait_ge(hi_ready, b + 1)
                nc.vector.tensor_tensor(m_lo[u][:], cols(u), m_hi[u][:].bitcast(F32), ALU.subtract).then_inc(lo_ready, 1)

            def rest_a(b, u):
                dve.wait_ge(hi_ready, b + (NB + 1))
                nc.vector.tensor_tensor(m_lo[u][:], ps_t[:], m_hi[u][:].bitcast(F32), ALU.subtract).then_inc(lo_ready, 1)

            def take_z(b, u):
                step = Chain(dve, zt_step, b)
                step(nc.vector.tensor_tensor(x_tile[u][:], v_hi[:, b, :].bitcast(F32), v_lo[:, b, :].bitcast(F32), ALU.add))
                dve.wait_ge(prod1_done, b + 1)
                nc.vector.scalar_tensor_tensor(out=x_norm[u][:], in0=ps_y[:, u, :], scalar=0.5, in1=x_tile[u][:],
                                               op0=ALU.mult, op1=ALU.add).then_inc(zt_ready, 1)
                dve.wait_ge(zhi_ready, b + 1)
                nc.vector.scalar_tensor_tensor(out=z_lo[:, b, :], in0=x_norm[u][:], scalar=dinv[:, bass.ds(b, 1)],
                                               in1=z_hi[:, b, :].bitcast(F32), op0=ALU.mult, op1=ALU.subtract).then_inc(z_ready, 1)

            sum_s(0, 0)
            rest_s(0, 0)

            def first(b, u):
                if exists(b + 1):
                    sum_s(b + 1, 1 - u)
                    rest_s(b + 1, 1 - u)
                else:
                    rest_a(0, 0)
                if exists(b - 1):
                    take_z(b - 1, 1 - u)
            pairs(dve, first)
            take_z(NB - 1, 1)

            dve.wait_ge(whi_ready, 2)
            nc.vector.tensor_tensor(w_part[1][:], w_raw[:], w_part[0][:].bitcast(F32), ALU.subtract).then_inc(w_ready, 1)
            nc.vector.tensor_tensor(wo_part[1][:], wo_raw[:], wo_part[0][:].bitcast(F32), ALU.subtract).then_inc(w_ready, 1)
            nc.vector.memset(s2_range[:], -3e38)

            def search(b, u):
                step = Chain(dve, top_step, b * 2)
                dve.wait_ge(rows_in[u], b * 8 + (16 - 8 * u + 16 * NB // 2))
                if exists(b - 1):
                    dve.wait_ge(top_kept, b)
                apart(dve)
                step(nc.vector.max(block_val[:], stage[u][:]))
                apart(dve)
                step(nc.vector.max_index(block_idx[:], block_val[:], stage[u][:]))
                nc.vector.tensor_copy(top_val[:, b, :], block_val[:]).then_inc(top_done, 1)
                nc.vector.tensor_copy(top_idx[:, b, :], block_idx[:]).then_inc(top_kept, 1)

            def norm(src, dst, step, ready, back, b):
                step(nc.vector.bn_stats(stats[:], src))
                apart(dve)
                step(nc.vector.bn_aggr(mean_var[:], stats[:]))
                nc.vector.tensor_scalar(var_eps[:], mean_var[:, 1:2], EPS, None, ALU.add).then_inc(ready, 1)
                dve.wait_ge(back, b + 1)
                return nc.vector.tensor_scalar(dst, src, mean_var[:, 0:1], rstd[:], ALU.subtract, ALU.mult)

            def take_x1(b, u):
                step = Chain(dve, norm_step, b * 3)
                dve.wait_ge(xt_in[u], b * 8 + 16 - 8 * u)
                dve.wait_ge(prod2_done, b + 1)
                step(nc.vector.tensor_tensor(x_tile[u][:], ps_y[:, u, :], x_tile[u][:], ALU.add))
                if exists(b - 2):
                    dve.wait_ge(x1_kept, b - 1)
                norm(x_tile[u][:], x_norm[u][:], step, var_ready, rstd_ready, b).then_inc(x1_ready, 1)

            def rest_t(b, u):
                dve.wait_ge(thi_ready, b + 1)
                nc.vector.tensor_tensor(t_lo[:], ps_x[:], t_hi[:].bitcast(F32), ALU.subtract).then_inc(t_ready, 1)

            def sum_scores(b, u):
                step = Chain(dve, tab_step, b * 3)
                dve.wait_ge(products_ready, b * 2 + 2)
                if exists(b - 1):
                    dve.wait_ge(tab_ready, b)
                step(nc.vector.tensor_reduce(s1[:, b, :], score_products[0][:].rearrange("p (h d) -> p h d", d=DH), AX.X, ALU.add))
                s2 = table_tile[u][:, D:ROW]
                if exists(b - 2):
                    dve.wait_ge(tab_out[u], b * 8 if u == 0 else b * 8 - 8)
                step(nc.vector.tensor_reduce(s2, score_products[1][:].rearrange("p (h d) -> p h d", d=DH), AX.X, ALU.add))
                step(nc.vector.tensor_tensor(s2_range[:, 0:H], s2_range[:, 0:H], s2, ALU.max))
                nc.vector.scalar_tensor_tensor(out=s2_range[:, H:2 * H], in0=s2, scalar=-1.0, in1=s2_range[:, H:2 * H],
                                               op0=ALU.mult, op1=ALU.max).then_inc(tab_ready, 1)

            search(0, 0)

            def second(b, u):
                if exists(b - 1):
                    take_x1(b - 1, 1 - u)
                if exists(b + 1):
                    rest_a(b + 1, 1 - u)
                if exists(b - 1):
                    rest_t(b - 1, 1 - u)
                if exists(b + 1):
                    search(b + 1, 1 - u)
                if exists(b - 1):
                    sum_scores(b - 1, 1 - u)
            pairs(dve, second)
            take_x1(NB - 1, 1)
            rest_t(NB - 1, 1)
            sum_scores(NB - 1, 1)

            nc.vector.memset(far[:], 0.0).then_inc(range_ready, 1)
            dve.wait_ge(range_all, 1)
            step = Chain(dve, far_step, 0)
            step(nc.vector.tensor_tensor(ssum[:], s2_all[:, 0:H], s2_all[:, H:2 * H], ALU.add))
            step(nc.vector.tensor_reduce(far[:, 0:1], ssum[:], AX.X, ALU.max))
            step(nc.vector.tensor_scalar(far[:, 1:2], far[:, 0:1], FAR, -1.0, ALU.add, ALU.mult))
            step(nc.vector.tensor_scalar(top_val[:], top_val[:], -1.0, 1.0, ALU.mult, ALU.add))
            step(nc.vector.tensor_scalar(top_val[:], top_val[:], MASK, None, ALU.mult))
            step(nc.vector.tensor_tensor(far_mask[:], top_val[:], top_val[:, :, 0:1].to_broadcast([P, NB, TOP]), ALU.subtract))
            step(nc.vector.tensor_scalar(far_mask[:], far_mask[:], far[:, 1:2], None, ALU.is_lt))
            step(nc.vector.scalar_tensor_tensor(out=top_val[:], in0=far_mask[:], scalar=-1e30, in1=top_val[:], op0=ALU.mult, op1=ALU.add))
            step(nc.vector.tensor_copy(idx_f[:], top_idx[:]))
            step(nc.vector.scalar_tensor_tensor(out=slot_idx[:], in0=far_mask[:], scalar=1e6, in1=idx_f[:], op0=ALU.mult, op1=ALU.add))
            step(nc.vector.tensor_scalar(needs[:, 1:1 + NB], far_mask[:, :, NARROW], -1.0, 1.0, ALU.mult, ALU.add))
            step(nc.vector.tensor_reduce(far[:, 0:1], far_mask[:, :, TOP - 1], AX.X, ALU.min))
            nc.vector.tensor_scalar(needs[:, 0:1], far[:, 0:1], -1.0, 1.0, ALU.mult, ALU.add).then_inc(needs_ready, 1)
            dve.wait_ge(needs_reduced, 1)
            nc.vector.tensor_copy(flags[:], needs_all[:]).then_inc(flags_ready, 1)

            def rest_hidden(path, b):
                dve.wait_ge(path.hi_ready, b + 1)
                nc.vector.tensor_tensor(t_lo[:], ps_x[:], t_hi[:].bitcast(F32), ALU.subtract).then_inc(path.lo_ready, 1)

            def finish(path, b, u):
                step = Chain(dve, path.tail_step, b * 5)
                dve.wait_ge(path.projected, b + 1)
                if exists(b - 2):
                    dve.wait_ge(path.out_done[u], b * 8 if u == 0 else b * 8 - 8)
                step(nc.vector.tensor_tensor(x_tile[u][:], ps_y[:, u, :], bob[:], ALU.add))
                nc.vector.tensor_scalar(x_norm[u][:], x_tile[u][:], 0.0, None, ALU.min).then_inc(path.min_ready, 1)
                dve.wait_ge(path.elu_exp, b + 1)
                step(nc.vector.scalar_tensor_tensor(out=x_tile[u][:], in0=x_tile[u][:], scalar=0.0, in1=x_norm[u][:],
                                                    op0=ALU.max, op1=ALU.add))
                step(nc.vector.scalar_tensor_tensor(out=x_tile[u][:], in0=x_tile[u][:], scalar=-1.0, in1=x1[:, b, :],
                                                    op0=ALU.add, op1=ALU.add))
                norm(x_tile[u][:], x_norm[u][:], step, path.var_ready, path.rstd_ready, b).then_inc(path.out_ready, 1)

            dve.wait_ge(flags_ready, 1)
            dve.wait_ge(x1_kept, NB)
            dve.wait_ge(small_in, 16 * (2 * H + 1))
            dense = dve.value_load(flags[0:1, 0:1], min_val=0, max_val=1)
            with dve.If(dense == 0):
                def indices(b, u):
                    nc.vector.tensor_copy(gather_idx[u][:], slot_idx[:, b, :]).then_inc(near.idx_ready, 1)

                def weigh_rows(b, u):
                    dve.wait_ge(near.got[u], (b + 2) * (8 * SLOTS) if u == 0 else (b + 1) * (8 * SLOTS))
                    step = Chain(dve, near.weigh_step, b * 7)
                    got = rows_got[u]
                    s1b = s1[:, b, :].rearrange("p (o h) -> p o h", o=1).to_broadcast([P, SLOTS, H])
                    mb = top_val[:, b, 0:SLOTS].rearrange("p (k o) -> p k o", o=1).to_broadcast([P, SLOTS, H])
                    step(nc.vector.tensor_tensor(scores[0][:], got[:, :, D:ROW], s1b, ALU.add))
                    step(nc.vector.scalar_tensor_tensor(out=scores[2][:], in0=scores[0][:], scalar=ALPHA, in1=scores[0][:],
                                                        op0=ALU.mult, op1=ALU.max))
                    step(nc.vector.tensor_tensor(scores[2][:], scores[2][:], mb, ALU.add))
                    step(nc.vector.tensor_reduce(smax[:], scores[2][:].rearrange("p k h -> p h k"), AX.X, ALU.max))
                    nc.vector.tensor_tensor(scores[0][:], scores[2][:], smax[:].rearrange("p (o h) -> p o h", o=1).to_broadcast([P, SLOTS, H]),
                                            ALU.subtract).then_inc(near.shifted, 1)
                    dve.wait_ge(near.exp_ready, b + 1)
                    step(nc.vector.tensor_reduce(ssum[:], scores[1][:].rearrange("p k h -> p h k"), AX.X, ALU.add))
                    step(nc.vector.reciprocal(ssum[:], ssum[:]))
                    step(nc.vector.tensor_tensor(scores[2][:], scores[1][:], ssum[:].rearrange("p (o h) -> p o h", o=1).to_broadcast([P, SLOTS, H]), ALU.mult))
                    if exists(b - 2):
                        dve.wait_ge(near.turned, b - 1)
                    nc.vector.tensor_tensor(
                        rows_weighted[u][:].rearrange("p k (h d) -> p (k h) d", d=DH),
                        got[:, :, 0:D].rearrange("p k (h d) -> p k h d", d=DH),
                        scores[2][:].rearrange("p k (h o) -> p k h o", o=1).to_broadcast([P, SLOTS, H, DH]), ALU.mult).then_inc(near.weighted, 1)

                indices(0, 0)
                indices(1, 1)

                def body(b, u):
                    weigh_rows(b, u)
                    if exists(b + 2):
                        dve.wait_ge(near.weighted, b + 1)
                        indices(b + 2, u)
                    if exists(b - 1):
                        rest_hidden(near, b - 1)
                    if exists(b - 2):
                        finish(near, b - 2, u)
                pairs(dve, body)
                rest_hidden(near, NB - 1)
                finish(near, NB - 2, 0)
                finish(near, NB - 1, 1)
            with dve.Else():
                dve.sem_inc(dense_block, 1)
                with dve.Fori(0, H) as h:
                    dve.wait_ge(head_in, h * 32 + 32)
                    apart(dve)
                    with dve.Fori(0, NB) as b:
                        t = h * NB + b
                        step = Chain(dve, dense_step, t * 6)
                        step(nc.vector.tensor_scalar(dense_score[:], dense_s2[:], s1[:, b, bass.ds(h, 1)], None, ALU.add))
                        step(nc.vector.scalar_tensor_tensor(out=dense_tmp[:], in0=dense_score[:], scalar=ALPHA, in1=dense_score[:],
                                                            op0=ALU.mult, op1=ALU.max))
                        dve.wait_ge(block_in, t * 16 + 16)
                        step(nc.vector.tensor_scalar(stage[0][:], stage[0][:], -1.0, 1.0, ALU.mult, ALU.add))
                        step(nc.vector.scalar_tensor_tensor(out=dense_score[:], in0=stage[0][:], scalar=MASK, in1=dense_tmp[:],
                                                            op0=ALU.mult, op1=ALU.add))
                        step(nc.vector.tensor_reduce(col[:, 0:1], dense_score[:], AX.X, ALU.max))
                        nc.vector.tensor_scalar(col[:, 1:2], col[:, 0:1], -1.0, None, ALU.mult).then_inc(dense_shifted, 1)
                        dve.wait_ge(dense_exp, t + 1)
                        step(nc.vector.reciprocal(col[:, 3:4], col[:, 2:3]))
                        dve.wait_ge(dense_prod, t + 1)
                        nc.vector.tensor_scalar(hidden[:, b, bass.ds(h * DH, DH)], ps_q[:, 0:DH], col[:, 3:4], None,
                                                ALU.mult).then_inc(dense_block, 1)
                dve.wait_ge(dense_block, H * NB + 1)

                def body(b, u):
                    if exists(b - 2):
                        dve.wait_ge(full.turned, b - 1)
                    nc.vector.tensor_copy(rows_weighted[u][:, 0, :], hidden[:, b, :]).then_inc(full.weighted, 1)
                    rest_hidden(full, b)
                    if exists(b - 1):
                        finish(full, b - 1, 1 - u)
                pairs(dve, body)
                finish(full, NB - 1, 1)
            dve.nop()

        @block.tensor
        def _(pe):
            pe.wait_ge(consts, 3)
            def col_sums(b, q, first):
                for k in range(NB):
                    mm = nc.tensor.matmul(ps_q[:, k:k + 1], stage[q][:, k * P:(k + 1) * P], ones[:],
                                          start=(first and k == 0), stop=(isinstance(b, int) and b == NB - 1), skip_group_check=True)
                mm.then_inc(col_summed, 1)
            for q in range(4):
                pe.wait_ge(first_in[q], 16)
                col_sums(q, q, q == 0)
            with pe.Fori(1, NB // 4) as g:
                for q in range(4):
                    pe.wait_ge(first_in[q], g * 16 + 16)
                    col_sums(g * 4 + q, q, False)

            def turn_adj(n, u):
                pe.wait_ge(rows_in[u], n * 8 + 16 - 8 * u)
                if not isinstance(n, int) or n >= 1:
                    if isinstance(n, int) and n > NB:
                        pe.wait_ge(lo_ready, n)
                    elif isinstance(n, int):
                        pe.wait_ge(s_summed, n)
                    else:
                        pe.wait_ge(ps_free[0], n)
                for k in range(NB):
                    mm = nc.tensor.transpose(ps_t[:, k, :], stage[u][:, k * P:(k + 1) * P], ident[:])
                mm.then_inc(turned, 1)

            ps_free = [None]

            def product(b, u, ks, hi, lo, last, done):
                for k in ks:
                    if done is prod1_done and isinstance(b, int) and b == 0:
                        pe.wait_ge(v_ready, k + 1)
                    if done is prod2_done and isinstance(b, int) and b == 0 and k in (0, NB - 1):
                        pe.wait_ge(z_ready, NB - 1 if k == 0 else NB)
                    for n, (m, v) in enumerate(((m_hi, hi), (m_hi, lo), (m_lo, hi))):
                        mm = nc.tensor.matmul(ps_y[:, u, :], m[u][:, k, :], v[:, k, :],
                                              start=(k == 0 and n == 0), stop=(k == NB - 1 and n == 2))
                if last:
                    mm.then_inc(done, 1)

            turn_adj(0, 0)
            ps_free[0] = s_summed

            def first(b, u):
                turn_adj(b + 1, 1 - u)
                pe.wait_ge(lo_ready, b + 1)
                if exists(b - 2):
                    pe.wait_ge(zt_ready, b - 1)
                product(b, u, range(NB), v_hi, v_lo, True, prod1_done)
            pairs(pe, first)
            ps_free[0] = lo_ready

            def turn_x1(b, u):
                pe.wait_ge(x1_ready, b + 1)
                if exists(b - 1):
                    pe.wait_ge(t_ready, b)
                for c in range(CT):
                    mm = nc.tensor.transpose(ps_x[:, c, :], x_norm[u][:, c * P:(c + 1) * P], ident[:])
                mm.then_inc(x1_turned, 1)

            def project(dst, w, done):
                for c in range(CT):
                    for n, (t, v) in enumerate(((t_hi, w[0]), (t_hi, w[1]), (t_lo, w[0]))):
                        mm = nc.tensor.matmul(dst, t[:, c, :], v[:, c, :], start=(c == 0 and n == 0), stop=(c == CT - 1 and n == 2))
                mm.then_inc(done, 1)

            def features(b):
                pe.wait_ge(t_ready, b + 1)
                if exists(b - 1):
                    pe.wait_ge(seq_copied, b)
                else:
                    pe.wait_ge(w_ready, 2)
                project(ps_q[:], w_part, seq_done)

            def second(b, u):
                if exists(b + 1):
                    turn_adj(b + (NB + 1), 1 - u)
                pe.wait_ge(lo_ready, b + (NB + 1))
                if exists(b - 2):
                    pe.wait_ge(x1_ready, b - 1)
                else:
                    pe.wait_ge(zt_ready, NB - 1 + b)
                product(b, u, range(0, 6), z_hi, z_lo, False, prod2_done)
                if exists(b - 1):
                    turn_x1(b - 1, 1 - u)
                product(b, u, range(6, 11), z_hi, z_lo, False, prod2_done)
                if exists(b - 1):
                    features(b - 1)
                product(b, u, range(11, NB), z_hi, z_lo, True, prod2_done)
            pairs(pe, second)
            turn_x1(NB - 1, 1)
            features(NB - 1)

            def turn_hidden(path, b, u, slots):
                pe.wait_ge(path.weighted, b + 1)
                if exists(b - 1):
                    pe.wait_ge(path.lo_ready, b)
                for c in range(CT):
                    for k in range(slots):
                        mm = nc.tensor.matmul(ps_x[:, c, :], rows_weighted[u][:, k, c * P:(c + 1) * P], ident[:],
                                              start=(k == 0), stop=(k == slots - 1))
                mm.then_inc(path.turned, 1)

            def project_out(path, b, u):
                pe.wait_ge(path.lo_ready, b + 1)
                if exists(b - 2):
                    pe.wait_ge(path.min_ready, b - 1)
                project(ps_y[:, u, :], wo_part, path.projected)

            pe.wait_ge(flags_ready, 1)
            dense = pe.value_load(flags[0:1, 0:1], min_val=0, max_val=1)
            with pe.If(dense == 0):
                def step(b, u):
                    turn_hidden(near, b, u, SLOTS)
                    if exists(b - 1):
                        project_out(near, b - 1, 1 - u)
                pairs(pe, step)
                project_out(near, NB - 1, 1)
            with pe.Else():
                with pe.Fori(0, H * NB) as t:
                    pe.wait_ge(dense_exp, t + 1)
                    for k in range(NB):
                        mm = nc.tensor.transpose(ps_t[:, k, :], dense_tmp[:, k * P:(k + 1) * P], ident[:])
                    mm.then_inc(dense_turned, 1)
                    pe.wait_ge(dense_copied, t + 1)
                    for k in range(NB):
                        mm = nc.tensor.matmul(ps_q[:, 0:DH], dense_pT[:, k, :], dense_seq[:, k, :], start=(k == 0), stop=(k == NB - 1))
                    mm.then_inc(dense_prod, 1)

                def step(b, u):
                    turn_hidden(full, b, u, 1)
                    project_out(full, b, u)
                pairs(pe, step)
            pe.nop()


_INS = ['x', 'adj', 'L1_gnn_W_seq', 'L1_gnn_a1', 'L1_gnn_a2', 'L1_gnn_W_out', 'L1_gnn_b_out']
_OUTS = [((2048, 512), 'float32')]


def kernel(**inputs):
    import numpy as _np
    import concourse.bacc as _bacc
    from concourse import mybir as _mybir
    from concourse.bass_utils import run_bass_kernel_spmd as _run

    nc = _bacc.Bacc("TRN2", target_bir_lowering=False, num_devices=1)
    arrays, args = {}, []
    for name in _INS:
        a = _np.ascontiguousarray(inputs[name])
        arrays[f"in_{name}_dram"] = a
        args.append(nc.dram_tensor(f"in_{name}_dram", a.shape, _mybir.dt.from_np(a.dtype), kind="ExternalInput").ap())
    for i, (shape, dtype) in enumerate(_OUTS):
        dt = _mybir.dt.from_np(_np.dtype(dtype))
        args.append(nc.dram_tensor(f"out_{i}_dram", shape, dt, kind="ExternalOutput").ap())
    graph_kernel(nc, *args)
    r = _run(nc, [arrays], core_ids=[0])
    got = tuple(r.results[0][f"out_{i}_dram"] for i in range(len(_OUTS)))
    return got[0]
```

```python
import concourse.bass as bass
from concourse import mybir
from contextlib import ExitStack

F32 = mybir.dt.float32
F32R = mybir.dt.float32r
I32 = mybir.dt.int32
U32 = mybir.dt.uint32
ALU = mybir.AluOpType
ACT = mybir.ActivationFunctionType
AX = mybir.AxisListType
RMAX = bass.bass_isa.ReduceOp.max

P = 128
N = 2048
D = 512
NB = N // P
CT = D // P
H = 16
DH = D // H
ROW = D + H
TOP = 8
SLOTS = TOP - 1
NARROW = 4
ALPHA = 0.2
MASK = -65500.0
FAR = 110.0
EPS = 1e-5


def pairs(eng, body, peeled=1):
    for b in range(2 * peeled):
        body(b, b % 2)
    with eng.Fori(peeled, NB // 2 - 1) as g:
        body(g * 2, 0)
        body(g * 2 + 1, 1)
    body(NB - 2, 0)
    body(NB - 1, 1)


def exists(b):
    return not isinstance(b, int) or 0 <= b < NB


class Chain:

    def __init__(self, eng, sem, done):
        self.eng, self.sem, self.done = eng, sem, done

    def __call__(self, step):
        self.add(step)
        self.wait()

    def add(self, step):
        step.then_inc(self.sem, 1)
        self.done = self.done + 1

    def wait(self):
        self.eng.wait_ge(self.sem, self.done)



def graph_kernel(nc, x, adj, w_seq, a1, a2, w_out, b_out, out):
    with ExitStack() as ctx:
        base = nc.sbuf_base + (-nc.sbuf_base) % 64
        K = 1024

        def at(name, offset, shape, dtype=F32):
            return nc.alloc_sbuf_tensor_at(name, shape, dtype, offset=base + offset)

        def psum(name, shape):
            return ctx.enter_context(nc.psum_tensor(name, shape, F32))

        def sem(name):
            return ctx.enter_context(nc.semaphore(name))

        v_hi = at("v_hi", 0, [P, NB, D], F32R)
        v_lo = at("v_lo", 32 * K, [P, NB, D], F32R)
        w_part = [at("w_hi", 0, [P, CT, D], F32R), at("w_lo", 8 * K, [P, CT, D], F32R)]
        ht_hi = [at(f"ht_hi{u}", 4 * u * K, [P, CT, P], F32R) for u in range(2)]
        ht_lo = [at(f"ht_lo{u}", (4 * u + 2) * K, [P, CT, P], F32R) for u in range(2)]
        wo_part = [at("wo_hi", 16 * K, [P, CT, D], F32R), at("wo_lo", 24 * K, [P, CT, D], F32R)]
        x1 = at("x1", 32 * K, [P, NB, D])
        w_raw = at("w_raw", 48 * K, [P, CT, D])
        wo_raw = at("wo_raw", 56 * K, [P, CT, D])
        xs = at("xs", 64 * K, [P, NB, D])
        z_hi = at("z_hi", 64 * K, [P, NB, D], F32R)
        z_lo = at("z_lo", 96 * K, [P, NB, D], F32R)
        rows_got = [at(f"rows_got{u}", (160, 128)[u] * K, [P, SLOTS, ROW]) for u in range(2)]
        rows_weighted = [at(f"rows_weighted{u}", 96 * K + u * 15 * K, [P, SLOTS, D]) for u in range(2)]
        hidden = at("hidden", 64 * K, [P, NB, D])
        stage = [at(f"stage{q}", (128 + 8 * q) * K, [P, N]) for q in range(4)]
        small = 144 * K
        a1b = at("a1b", small, [P, D])
        a2b = at("a2b", small + 2 * K, [P, D])
        bob = at("bob", small + 4 * K, [P, D])
        score_products = [at(f"score_products{i}", small + (6 + 2 * i) * K, [P, D]) for i in range(2)]
        table_tile = [at(f"table_tile{u}", small + 10 * K + u * 2112, [P, ROW]) for u in range(2)]
        top_val = at("top_val", small + 10 * K + 4224, [P, NB, TOP])
        top_idx = at("top_idx", small + 10 * K + 4736, [P, NB, TOP], U32)
        gather_idx = [at(f"gather_idx{u}", small + 10 * K + 5248 + 32 * u, [P, TOP], U32) for u in range(2)]
        ones_row = at("ones_row", small + 10 * K + 5376, [P, P], F32R)
        b_part = [at("b_hi", small + 6 * K, [P, D], F32R), at("b_lo", small + 8 * K, [P, D], F32R)]
        behind = 4 * SLOTS * ROW
        scores = [at(f"scores{i}", 160 * K + behind + i * 512, [P, SLOTS, H]) for i in range(3)]
        far_mask = at("far_mask", 128 * K + behind, [P, NB, TOP])
        idx_f = at("idx_f", 128 * K + behind + 512, [P, NB, TOP])
        slot_idx = at("slot_idx", 128 * K + behind + 1024, [P, NB, TOP], U32)
        m_hi = [at(f"m_hi{u}", (160 + 16 * u) * K, [P, NB, P], F32R) for u in range(2)]
        m_lo = [at(f"m_lo{u}", (168 + 16 * u) * K, [P, NB, P], F32R) for u in range(2)]
        col_partial = at("col_partial", 168 * K, [P, N])
        dense_s2 = at("dense_s2", 160 * K, [P, N])
        dense_score = at("dense_score", 168 * K, [P, N])
        dense_tmp = at("dense_tmp", 176 * K, [P, N])
        dense_pT = at("dense_pT", 184 * K, [P, NB, P])
        dense_seq = at("dense_seq", 136 * K, [P, NB, DH])
        x_tile = [at(f"x_tile{u}", (192 + 2 * u) * K, [P, D]) for u in range(2)]
        x_norm = [at(f"x_norm{u}", (196 + 2 * u) * K, [P, D]) for u in range(2)]
        t_hi = at("t_hi", 200 * K, [P, CT, P], F32R)
        t_lo = at("t_lo", 202 * K, [P, CT, P], F32R)
        ident = at("ident", 204 * K, [P, P])
        s1 = at("s1", 204 * K + 512, [P, NB, H])
        tail = [205 * K + 512]

        def little(name, shape, dtype=F32):
            size = 4
            for s in shape[1:]:
                size *= s
            tail[0] += size + -size % 32
            return at(name, tail[0] - size - -size % 32, shape, dtype)

        ones = little("ones", [P, 1])
        row_sum = little("row_sum", [P, NB])
        deg = little("deg", [P, NB])
        deg_pos = little("deg_pos", [P, NB])
        neg_half = little("neg_half", [P, NB])
        deg_pow = little("deg_pow", [P, NB])
        dinv = little("dinv", [P, NB])
        stats = little("stats", [P, 6])
        minus_one = little("minus_one", [P, 1])
        neg_mean = little("neg_mean", [P, 1])
        shift = [little(f"shift{u}", [P, 1]) for u in range(2)]
        mean_var = [little(f"mean_var{u}", [P, 2]) for u in range(2)]
        var_eps = [little(f"var_eps{u}", [P, 1]) for u in range(2)]
        rstd = [little(f"rstd{u}", [P, 1]) for u in range(2)]
        extent = little("extent", [P, 2 * H + 1 + NB])
        extent_all = little("extent_all", [P, 2 * H + 1 + NB])
        far = little("far", [P, 2])
        flags = little("flags", [P, 1 + NB], I32)
        block_val = little("block_val", [P, TOP])
        block_idx = little("block_idx", [P, TOP], U32)
        smax = little("smax", [P, H])
        ssum = little("ssum", [P, H])
        col = little("col", [P, 4])

        ps_t = psum("ps_t", [P, NB, P])
        ps_y = psum("ps_y", [P, 2, D])
        ps_x = psum("ps_x", [P, CT, P])
        ps_q = psum("ps_q", [P, D])
        ps_h = [ps_x, ps_t]

        table = nc.dram_tensor("table", [N, ROW], F32).ap()
        s2_rows = nc.dram_tensor("s2_rows", [H, N], F32).ap()

        x_b = x.rearrange("(b p) d -> b p d", p=P)
        out_b = out.rearrange("(b p) d -> b p d", p=P)
        adj_b = adj.rearrange("(b p) j -> b p j", p=P)
        adj_c = adj.rearrange("(k p) (b i) -> b p k i", p=P, i=P)
        table_b = table.rearrange("(b p) d -> b p d", p=P)
        w_v = w_seq.rearrange("(c p) d -> p c d", p=P)
        wo_v = w_out.rearrange("(c p) d -> p c d", p=P)

        def row_of(v):
            return v.rearrange("(a d) -> a d", a=1).to_broadcast([P, v.shape[0]])

        x_in = [sem(f"x_in{i}") for i in range(4)]
        first_in = [sem(f"first_in{q}") for q in range(4)]
        consts = sem("consts")
        col_added = sem("col_added")
        col_summed = sem("col_summed")
        row_summed = sem("row_summed")
        deg_step = sem("deg_step")
        deg_ready = sem("deg_ready")
        pow_ready = sem("pow_ready")
        dinv_ready = sem("dinv_ready")
        vhi_ready = sem("vhi_ready")
        v_ready = sem("v_ready")
        rows_in = [sem(f"rows_in{u}") for u in range(2)]
        cols_in = [sem(f"cols_in{u}") for u in range(2)]
        turned = sem("turned")
        s_summed = sem("s_summed")
        hi_ready = sem("hi_ready")
        lo_ready = sem("lo_ready")
        prod1_done = sem("prod1_done")
        zt_step = sem("zt_step")
        zt_ready = sem("zt_ready")
        zhi_ready = sem("zhi_ready")
        z_ready = sem("z_ready")
        small_in = sem("small_in")
        w_in = sem("w_in")
        whi_ready = sem("whi_ready")
        w_ready = sem("w_ready")
        xt_in = [sem(f"xt_in{u}") for u in range(2)]
        prod2_done = sem("prod2_done")
        norm_step = sem("norm_step")
        var_ready = sem("var_ready")
        rstd_ready = sem("rstd_ready")
        x1_ready = sem("x1_ready")
        x1_kept = sem("x1_kept")
        x1_turned = sem("x1_turned")
        thi_ready = sem("thi_ready")
        t_ready = sem("t_ready")
        seq_done = sem("seq_done")
        seq_copied = sem("seq_copied")
        products_ready = sem("products_ready")
        tab_step = sem("tab_step")
        tab_ready = sem("tab_ready")
        tab_out = [sem(f"tab_out{u}") for u in range(2)]
        top_step = sem("top_step")
        top_done = sem("top_done")
        top_kept = sem("top_kept")
        range_ready = sem("range_ready")
        range_all = sem("range_all")
        far_step = sem("far_step")
        flags_ready = sem("flags_ready")
        table_done = sem("table_done")
        got_clear = sem("got_clear")
        bias_hi_ready = sem("bias_hi_ready")
        bias_ready = sem("bias_ready")
        passed = sem("passed")

        class Path:

            def __init__(self, name):
                self.idx_ready = sem(name + "idx_ready")
                self.got = [sem(name + f"got{u}") for u in range(2)]
                self.weigh_step = sem(name + "weigh_step")
                self.shifted = sem(name + "shifted")
                self.exp_ready = sem(name + "exp_ready")
                self.weighted = sem(name + "weighted")
                self.turned = sem(name + "turned")
                self.hi_ready = sem(name + "hi_ready")
                self.lo_ready = sem(name + "lo_ready")
                self.projected = sem(name + "projected")
                self.tail_step = sem(name + "tail_step")
                self.relu_ready = sem(name + "relu_ready")
                self.elu_exp = sem(name + "elu_exp")
                self.var_ready = sem(name + "var_ready")
                self.rstd_step = sem(name + "rstd_step")
                self.rstd_ready = sem(name + "rstd_ready")
                self.out_ready = sem(name + "out_ready")
                self.out_done = [sem(name + f"out_done{u}") for u in range(2)]

        near = Path("near_")
        full = Path("full_")
        s2_turned = sem("s2_turned")
        head_in = sem("head_in")
        block_in = sem("block_in")
        dense_step = sem("dense_step")
        dense_shifted = sem("dense_shifted")
        dense_exp = sem("dense_exp")
        dense_turned = sem("dense_turned")
        dense_copied = sem("dense_copied")
        dense_prod = sem("dense_prod")
        dense_block = sem("dense_block")

        def apart(eng):
            eng.sem_inc(passed, 1)

        first_rest = (slice(0, 4), slice(4, NB))

        block = ctx.enter_context(nc.Block())

        @block.sync
        def _(sp):
            for q in range(4):
                sp.dma_start(stage[q][:], adj_b[q]).then_inc(first_in[q], 16)
            with sp.Fori(1, NB // 4) as g:
                for q in range(4):
                    sp.wait_ge(col_added, g * 4 + (q - 3))
                    sp.wait_ge(row_summed, g * 4 + (q - 3))
                    sp.dma_start(stage[q][:], adj_b[g * 4 + q]).then_inc(first_in[q], 16)

            def load_rows(n, b, u):
                sp.dma_start(stage[u][:], adj_b[b]).then_inc(rows_in[u], 16)

            def load_cols(b, u):
                sp.dma_start(stage[2 + u][:].rearrange("p (k i) -> p k i", i=P), adj_c[b]).then_inc(cols_in[u], 16)

            x_parts = x.rearrange("(b p) d -> p b d", p=P)

            def buffer_read(q):
                sp.wait_ge(col_added, NB - 3 + q)
                sp.wait_ge(row_summed, NB - 3 + q)

            def load_x(i):
                sp.dma_start(xs[:, 4 * i:4 * i + 4, :], x_parts[:, 4 * i:4 * i + 4, :]).then_inc(x_in[i], 16)
            buffer_read(0)
            load_rows(0, 0, 0)
            load_x(0)
            buffer_read(2)
            load_cols(0, 0)
            load_rows(1, 1, 1)
            load_x(1)
            load_x(2)
            buffer_read(3)
            load_cols(1, 1)
            load_x(3)

            def first(b, u):
                sp.wait_ge(turned, b + 1)
                apart(sp)
                if isinstance(b, int) and b + 2 >= NB:
                    load_rows(b + 2, b + 2 - NB, u)
                else:
                    load_rows(b + 2, b + 2, u)
                    sp.wait_ge(lo_ready, b + 1)
                    load_cols(b + 2, u)
            pairs(sp, first)

            def next_rows(b, u):
                sp.wait_ge(turned, b + (NB + 1))
                apart(sp)
                sp.wait_ge(top_done, b + 1)
                load_rows(b + 2 + NB, b + 2, u)
            next_rows(0, 0)

            sp.wait_ge(z_ready, NB)
            for u in range(2):
                sp.dma_start(x_tile[u][:], x_b[u]).then_inc(xt_in[u], 16)
            sp.dma_start(w_raw[:], w_v).then_inc(w_in, 16)
            sp.dma_start(wo_raw[:], wo_v).then_inc(w_in, 16)
            for vec, tile in ((a1, a1b), (a2, a2b)):
                sp.dma_start(tile[:].rearrange("p (h d) -> p h d", d=DH),
                             vec.rearrange("(a b d) -> a b d", a=1, b=1).to_broadcast([P, H, DH])).then_inc(small_in, 16)
            sp.dma_start(bob[:], row_of(b_out)).then_inc(small_in, 16)

            def store_table(b, u):
                sp.wait_ge(tab_ready, b + 1)
                sp.dma_start(table_b[b], table_tile[u][:]).then_inc(tab_out[u], 16)

            def second(b, u):
                if not isinstance(b, int) or 1 <= b < NB - 2:
                    next_rows(b, u)
                if not isinstance(b, int) or 1 <= b < NB - 1:
                    sp.wait_ge(x1_ready, b)
                    sp.dma_start(x_tile[1 - u][:], x_b[b + 1]).then_inc(xt_in[1 - u], 16)
                if exists(b - 1):
                    store_table(b - 1, 1 - u)
            pairs(sp, second)
            store_table(NB - 1, 1)
            for u in range(2):
                sp.wait_ge(tab_out[u], 16 * NB // 2)
            sp.sem_inc(table_done, 1)

            def store_out(path):
                def store(b, u):
                    sp.wait_ge(path.out_ready, b + 1)
                    sp.dma_start(out_b[b], x_norm[u][:]).then_inc(path.out_done[u], 16)
                pairs(sp, store)
                for u in range(2):
                    sp.wait_ge(path.out_done[u], 16 * NB // 2)

            sp.wait_ge(flags_ready, 1)
            dense = sp.value_load(flags[0:1, 0:1], min_val=0, max_val=1)
            with sp.If(dense == 0):
                store_out(near)
            with sp.Else():
                with nc.allow_non_contiguous_dma(reason="neighbour scores by head, once"):
                    sp.dma_start(s2_rows.rearrange("h (j o) -> h j o", o=1),
                                 table[:, D:ROW].rearrange("j (h o) -> h j o", o=1)).then_inc(s2_turned, 16)
                sp.wait_ge(s2_turned, 16)
                with sp.Fori(0, H) as h:
                    sp.wait_ge(dense_block, h * NB + 1)
                    sp.dma_start(dense_s2[:], row_of(s2_rows[h])).then_inc(head_in, 16)
                    sp.dma_start(dense_seq[:], table[:, bass.ds(h * DH, DH)].rearrange("(k p) d -> p k d", p=P)).then_inc(head_in, 16)
                    with sp.Fori(0, NB) as b:
                        sp.wait_ge(dense_block, h * NB + b + 1)
                        sp.dma_start(stage[0][:], adj_b[b]).then_inc(block_in, 16)
                store_out(full)
            sp.nop()

        @block.gpsimd
        def _(pool):
            nc.gpsimd.memset(ident[:], 0.0).then_inc(consts, 1)
            nc.gpsimd.memset(neg_half[:], -0.5)
            nc.gpsimd.memset(minus_one[:], -1.0)
            nc.gpsimd.memset(ones[:], 1.0).then_inc(consts, 1)
            pool.wait_ge(consts, 2)
            nc.gpsimd.affine_select(out=ident[:], in_=ident[:], compare_op=ALU.not_equal, fill=1.0, base=0,
                                    pattern=[[-1, P]], channel_multiplier=1).then_inc(consts, 1)
            pool.wait_ge(deg_ready, 1)
            for ks in first_rest:
                nc.gpsimd.tensor_tensor(deg_pow[:, ks], deg_pos[:, ks], neg_half[:, ks], ALU.pow).then_inc(pow_ready, 1)

            def inv_std(ready, done, b, u):
                pool.wait_ge(ready, b + 1)
                nc.gpsimd.tensor_tensor(rstd[u][:], var_eps[u][:], neg_half[:, 0:1], ALU.pow).then_inc(done, 1)

            def second(b, u):
                if exists(b - 1):
                    inv_std(var_ready, rstd_ready, b - 1, 1 - u)
                    if not exists(b + 1):
                        clear_rows()
                    products(b - 1, 1 - u)

            def clear_rows():
                pool.wait_ge(prod2_done, NB - 1)
                nc.gpsimd.memset(rows_got[0][:], 0.0).then_inc(got_clear, 1)
                pool.wait_ge(turned, 2 * NB)
                pool.wait_ge(top_done, NB)
                nc.gpsimd.memset(rows_got[1][:], 0.0).then_inc(got_clear, 1)

            def products(b, u):
                pool.wait_ge(seq_copied, b + 1)
                if exists(b - 1):
                    pool.wait_ge(tab_ready, b)
                else:
                    pool.wait_ge(small_in, 16 * 3)
                if exists(b + 1):
                    nc.gpsimd.tensor_tensor(score_products[0][:], table_tile[u][:, 0:D], a1b[:],
                                            ALU.mult).then_inc(products_ready, 1)
                nc.gpsimd.tensor_tensor(score_products[1][:], table_tile[u][:, 0:D], a2b[:], ALU.mult).then_inc(products_ready, 1)
            pairs(pool, second)
            inv_std(var_ready, rstd_ready, NB - 1, 1)
            products(NB - 1, 1)
            pool.wait_ge(range_ready, 1)
            nc.gpsimd.partition_all_reduce(extent_all[:], extent[:], P, RMAX).then_inc(range_all, 1)

            def inv_std_shift(path, b, u):
                inv_std(path.var_ready, path.rstd_step, b, u)
                nc.gpsimd.tensor_tensor(neg_mean[:], mean_var[u][:, 0:1], minus_one[:], ALU.mult).then_inc(path.rstd_step, 1)
                pool.wait_ge(path.rstd_step, b * 2 + 2)
                nc.gpsimd.tensor_tensor(shift[u][:], neg_mean[:], rstd[u][:], ALU.mult).then_inc(path.rstd_ready, 1)
                pool.wait_ge(path.rstd_ready, b + 1)

            pool.wait_ge(flags_ready, 1)
            pool.wait_ge(table_done, 1)
            dense = pool.value_load(flags[0:1, 0:1], min_val=0, max_val=1)
            with pool.If(dense == 0):
                def gather(b, u):
                    if exists(b - 2):
                        pool.wait_ge(near.weighted, b - 1)
                        nc.gpsimd.tensor_copy(gather_idx[u][:], slot_idx[:, b, :]).then_inc(near.idx_ready, 1)
                    pool.wait_ge(near.idx_ready, b + 1)
                    apart(pool)
                    for k in range(NARROW - 1):
                        fetch(k, u, 16)
                    wide = pool.value_load(flags[0:1, bass.ds(b + 1, 1)], min_val=0, max_val=1)
                    with pool.If(wide == 0):
                        fetch(NARROW - 1, u, 16 * (SLOTS - NARROW + 1))
                    with pool.Else():
                        for k in range(NARROW - 1, SLOTS):
                            fetch(k, u, 16)

                def fetch(k, u, add):
                    nc.gpsimd.indirect_dma_start(
                        out=rows_got[u][:, k, :], out_offset=None, in_=table,
                        in_offset=bass.IndirectOffsetOnAxis(ap=gather_idx[u][:, k:k + 1], axis=0),
                        bounds_check=N - 1, oob_is_err=False).then_inc(near.got[u], add)

                def step(b, u):
                    if exists(b + 1):
                        gather(b + 1, 1 - u)
                    if exists(b - 3):
                        inv_std_shift(near, b - 3, 1 - u)
                pool.wait_ge(got_clear, 2)
                gather(0, 0)
                pairs(pool, step, peeled=2)
                inv_std_shift(near, NB - 3, 1)
                inv_std_shift(near, NB - 2, 0)
                inv_std_shift(near, NB - 1, 1)
            with pool.Else():
                def step(b, u):
                    if exists(b - 1):
                        inv_std_shift(full, b - 1, 1 - u)
                pairs(pool, step)
                inv_std_shift(full, NB - 1, 1)
            pool.nop()

        @block.scalar
        def _(act):
            def sum_rows(b, q, loaded):
                act.wait_ge(first_in[q], loaded)
                if not isinstance(b, int) or b > 0:
                    act.wait_ge(row_summed, b)
                nc.scalar.activation(ps_t[:].rearrange("p k i -> p (k i)"), stage[q][:], ACT.Copy,
                                     accum_out=row_sum[:, bass.ds(b, 1)]).then_inc(row_summed, 1)
            for q in range(4):
                sum_rows(q, q, 16)
            with act.Fori(1, NB // 4) as g:
                for q in range(4):
                    sum_rows(g * 4 + q, q, g * 16 + 16)
            def lead_s(b, u):
                act.wait_ge(s_summed, b + 1)
                if exists(b - 2):
                    act.wait_ge(prod1_done, b - 1)
                nc.scalar.copy(m_hi[u][:], stage[2 + u][:].rearrange("p (k i) -> p k i", i=P)).then_inc(hi_ready, 1)

            act.wait_ge(dinv_ready, 1)
            for k in range(NB):
                if k == 3:
                    lead_s(0, 0)
                if k == 4:
                    act.wait_ge(dinv_ready, 2)
                if k % 4 == 0:
                    act.wait_ge(x_in[k // 4], 16)
                nc.scalar.activation(v_hi[:, k, :], xs[:, k, :], ACT.Copy, scale=dinv[:, k:k + 1]).then_inc(vhi_ready, 1)

            def lead_a(b, u):
                act.wait_ge(turned, b + (NB + 1))
                if exists(b - 2):
                    act.wait_ge(prod2_done, b - 1)
                else:
                    act.wait_ge(prod1_done, NB - 1 + b)
                nc.scalar.copy(m_hi[u][:], ps_t[:]).then_inc(hi_ready, 1)

            def lead_z(b, u):
                act.wait_ge(zt_ready, b + 1)
                nc.scalar.activation(z_hi[:, b, :], x_norm[u][:], ACT.Copy, scale=dinv[:, bass.ds(b, 1)]).then_inc(zhi_ready, 1)

            def first(b, u):
                if exists(b + 1):
                    lead_s(b + 1, 1 - u)
                else:
                    lead_a(0, 0)
                if exists(b - 1):
                    lead_z(b - 1, 1 - u)
            pairs(act, first)
            lead_z(NB - 1, 1)

            def keep(b, u):
                act.wait_ge(x1_turned, b + 1)
                if exists(b - 1):
                    act.wait_ge(seq_done, b)
                nc.scalar.copy(t_hi[:], ps_x[:]).then_inc(thi_ready, 1)
                if not exists(b - 1):
                    act.wait_ge(w_ready, 2)
                nc.scalar.activation(x1[:, b, :], x_norm[u][:], ACT.Copy, bias=-1.0).then_inc(x1_kept, 1)
                act.wait_ge(seq_done, b + 1)
                if exists(b - 2):
                    act.wait_ge(tab_out[u], b * 8 if u == 0 else b * 8 - 8)
                nc.scalar.copy(table_tile[u][:, 0:D], ps_q[:]).then_inc(seq_copied, 1)

            def second(b, u):
                if exists(b + 1):
                    lead_a(b + 1, 1 - u)
                if isinstance(b, int) and b == 1:
                    act.wait_ge(w_in, 32)
                    nc.scalar.copy(w_part[0][:], w_raw[:]).then_inc(whi_ready, 1)
                    nc.scalar.copy(wo_part[0][:], wo_raw[:]).then_inc(whi_ready, 1)
                if exists(b - 1):
                    keep(b - 1, 1 - u)
            pairs(act, second, peeled=2)
            keep(NB - 1, 1)
            act.wait_ge(small_in, 16 * 3)
            act.wait_ge(tab_ready, NB)
            nc.scalar.copy(b_part[0][:], bob[:]).then_inc(bias_hi_ready, 1)
            nc.scalar.activation(ones_row[:], ident[:], ACT.Copy, scale=0.0, bias=1.0).then_inc(bias_ready, 1)

            def lead_hidden(path, b, u):
                act.wait_ge(path.turned, b + 1)
                if exists(b - 2):
                    act.wait_ge(path.projected, b - 1)
                nc.scalar.copy(ht_hi[u][:], ps_h[u][:, 0:CT, :]).then_inc(path.hi_ready, 1)

            def elu_exp(path, b, u):
                if exists(b - 2):
                    act.wait_ge(path.out_done[u], b * 8 if u == 0 else b * 8 - 8)
                act.wait_ge(path.projected, b + 1)
                nc.scalar.activation(x_norm[u][:], ps_y[:, u, :], ACT.Exp).then_inc(path.elu_exp, 1)

            def normed_out(path, b, u):
                act.wait_ge(path.rstd_ready, b + 1)
                nc.scalar.activation(x_norm[u][:], x_tile[u][:], ACT.Identity, bias=shift[u][:],
                                     scale=rstd[u][:]).then_inc(path.out_ready, 1)

            act.wait_ge(flags_ready, 1)
            dense = act.value_load(flags[0:1, 0:1], min_val=0, max_val=1)
            with act.If(dense == 0):
                def exp_slots(b):
                    act.wait_ge(near.shifted, b + 1)
                    nc.scalar.activation(scores[1][:], scores[0][:], ACT.Exp).then_inc(near.exp_ready, 1)

                def step(b, u):
                    exp_slots(b)
                    if exists(b - 1):
                        lead_hidden(near, b - 1, 1 - u)
                    if exists(b - 2):
                        elu_exp(near, b - 2, u)
                    if exists(b - 3):
                        normed_out(near, b - 3, 1 - u)
                pairs(act, step, peeled=2)
                lead_hidden(near, NB - 1, 1)
                elu_exp(near, NB - 2, 0)
                normed_out(near, NB - 3, 1)
                elu_exp(near, NB - 1, 1)
                normed_out(near, NB - 2, 0)
                normed_out(near, NB - 1, 1)
            with act.Else():
                with act.Fori(0, H * NB) as t:
                    act.wait_ge(dense_shifted, t + 1)
                    nc.scalar.activation(dense_tmp[:], dense_score[:], ACT.Exp, bias=col[:, 1:2],
                                         accum_out=col[:, 2:3]).then_inc(dense_exp, 1)
                    act.wait_ge(dense_turned, t + 1)
                    nc.scalar.copy(dense_pT[:], ps_t[:]).then_inc(dense_copied, 1)

                def step(b, u):
                    lead_hidden(full, b, u)
                    if exists(b - 1):
                        elu_exp(full, b - 1, 1 - u)
                    if exists(b - 2):
                        normed_out(full, b - 2, u)
                pairs(act, step, peeled=2)
                elu_exp(full, NB - 1, 1)
                normed_out(full, NB - 2, 0)
                normed_out(full, NB - 1, 1)
            act.nop()

        @block.vector
        def _(dve):
            def cols(u):
                return stage[2 + u][:].rearrange("p (k i) -> p k i", i=P)

            def sum_s(b, u):
                dve.wait_ge(turned, b + 1)
                dve.wait_ge(cols_in[u], b * 8 + 16 - 8 * u)
                nc.vector.tensor_tensor(cols(u), ps_t[:], cols(u), ALU.add).then_inc(s_summed, 1)

            def rest_s(b, u):
                dve.wait_ge(hi_ready, b + 1)
                nc.vector.tensor_tensor(m_lo[u][:], cols(u), m_hi[u][:].bitcast(F32), ALU.subtract).then_inc(lo_ready, 1)

            dve.wait_ge(first_in[0], 16)
            nc.vector.tensor_copy(col_partial[:], stage[0][:]).then_inc(col_added, 1)

            def add_block(b, q, loaded):
                dve.wait_ge(first_in[q], loaded)
                dve.wait_ge(col_added, b)
                nc.vector.tensor_tensor(col_partial[:], col_partial[:], stage[q][:], ALU.add).then_inc(col_added, 1)
            for q in range(1, 4):
                add_block(q, q, 16)
            with dve.Fori(1, NB // 4) as g:
                for q in range(4):
                    add_block(g * 4 + q, q, g * 16 + 16)
            dve.wait_ge(row_summed, NB)
            dve.wait_ge(col_summed, 1)
            step = Chain(dve, deg_step, 0)
            step(nc.vector.tensor_tensor(deg[:], ps_q[:, 0:NB], row_sum[:], ALU.add))
            step(nc.vector.tensor_scalar(deg[:], deg[:], 0.5, 1.0, ALU.mult, ALU.add))
            nc.vector.tensor_scalar(deg_pos[:], deg[:], 1.2e-38, None, ALU.max).then_inc(deg_ready, 1)

            def take_dinv(part):
                dve.wait_ge(pow_ready, part + 1)
                ks = first_rest[part]
                nc.vector.scalar_tensor_tensor(out=dinv[:, ks], in0=deg[:, ks], scalar=0.0, in1=deg_pow[:, ks],
                                               op0=ALU.is_gt, op1=ALU.mult).then_inc(dinv_ready, 1)
                dve.wait_ge(dinv_ready, part + 1)

            def rest_v(k):
                dve.wait_ge(vhi_ready, k + 1)
                nc.vector.scalar_tensor_tensor(out=v_lo[:, k, :], in0=xs[:, k, :], scalar=dinv[:, bass.ds(k, 1)],
                                               in1=v_hi[:, k, :].bitcast(F32), op0=ALU.mult, op1=ALU.subtract).then_inc(v_ready, 1)
            take_dinv(0)
            rest_v(0)
            rest_v(1)
            sum_s(0, 0)
            take_dinv(1)
            rest_v(2)
            rest_s(0, 0)
            with dve.Fori(3, NB // 2) as k:
                rest_v(k)
            sum_s(1, 1)
            with dve.Fori(NB // 2, NB) as k:
                rest_v(k)

            def rest_a(b, u):
                dve.wait_ge(hi_ready, b + (NB + 1))
                nc.vector.tensor_tensor(m_lo[u][:], ps_t[:], m_hi[u][:].bitcast(F32), ALU.subtract).then_inc(lo_ready, 1)

            def take_z(b, u):
                step = Chain(dve, zt_step, b)
                step(nc.vector.tensor_tensor(x_tile[u][:], v_hi[:, b, :].bitcast(F32), v_lo[:, b, :].bitcast(F32), ALU.add))
                dve.wait_ge(prod1_done, b + 1)
                nc.vector.scalar_tensor_tensor(out=x_norm[u][:], in0=ps_y[:, u, :], scalar=0.5, in1=x_tile[u][:],
                                               op0=ALU.mult, op1=ALU.add).then_inc(zt_ready, 1)
                dve.wait_ge(zhi_ready, b + 1)
                nc.vector.scalar_tensor_tensor(out=z_lo[:, b, :], in0=x_norm[u][:], scalar=dinv[:, bass.ds(b, 1)],
                                               in1=z_hi[:, b, :].bitcast(F32), op0=ALU.mult, op1=ALU.subtract).then_inc(z_ready, 1)

            def first(b, u):
                if exists(b + 1):
                    if exists(b - 1):
                        sum_s(b + 1, 1 - u)
                    rest_s(b + 1, 1 - u)
                else:
                    rest_a(0, 0)
                if exists(b - 1):
                    take_z(b - 1, 1 - u)
            pairs(dve, first)
            nc.vector.memset(extent[:], -3e38)

            def search(b, u):
                step = Chain(dve, top_step, b * 2)
                dve.wait_ge(rows_in[u], b * 8 + (16 - 8 * u + 16 * NB // 2))
                if exists(b - 1):
                    dve.wait_ge(top_kept, b)
                apart(dve)
                step(nc.vector.max(block_val[:], stage[u][:]))
                apart(dve)
                step(nc.vector.max_index(block_idx[:], block_val[:], stage[u][:]))
                nc.vector.tensor_copy(top_val[:, b, :], block_val[:]).then_inc(top_done, 1)
                nc.vector.tensor_copy(top_idx[:, b, :], block_idx[:]).then_inc(top_kept, 1)

            search(0, 0)
            take_z(NB - 1, 1)

            def deviations(src, u, step, ready):
                step(nc.vector.bn_stats(stats[:], src))
                apart(dve)
                step(nc.vector.bn_aggr(mean_var[u][:], stats[:]))
                nc.vector.tensor_scalar(var_eps[u][:], mean_var[u][:, 1:2], EPS, None, ALU.add).then_inc(ready, 1)

            def normed(b, u, back):
                dve.wait_ge(back, b + 1)
                return nc.vector.tensor_scalar(x_norm[u][:], x_tile[u][:], mean_var[u][:, 0:1], rstd[u][:], ALU.subtract, ALU.mult)

            def take_x1(b, u):
                step = Chain(dve, norm_step, b * 3)
                dve.wait_ge(xt_in[u], b * 8 + 16 - 8 * u)
                dve.wait_ge(prod2_done, b + 1)
                step(nc.vector.tensor_tensor(x_tile[u][:], ps_y[:, u, :], x_tile[u][:], ALU.add))
                if exists(b - 2):
                    dve.wait_ge(x1_kept, b - 1)
                deviations(x_tile[u][:], u, step, var_ready)
                normed(b, u, rstd_ready).then_inc(x1_ready, 1)

            def rest_t(b, u):
                dve.wait_ge(thi_ready, b + 1)
                nc.vector.tensor_tensor(t_lo[:], ps_x[:], t_hi[:].bitcast(F32), ALU.subtract).then_inc(t_ready, 1)

            def sum_scores(b, u):
                step = Chain(dve, tab_step, b * 3)
                dve.wait_ge(products_ready, b * 2 + 2)
                if exists(b - 1):
                    dve.wait_ge(tab_ready, b)
                step(nc.vector.tensor_reduce(s1[:, b, :], score_products[0][:].rearrange("p (h d) -> p h d", d=DH), AX.X, ALU.add))
                s2 = table_tile[u][:, D:ROW]
                if exists(b - 2):
                    dve.wait_ge(tab_out[u], b * 8 if u == 0 else b * 8 - 8)
                step(nc.vector.tensor_reduce(s2, score_products[1][:].rearrange("p (h d) -> p h d", d=DH), AX.X, ALU.add))
                step(nc.vector.tensor_tensor(extent[:, 0:H], extent[:, 0:H], s2, ALU.max))
                nc.vector.scalar_tensor_tensor(out=extent[:, H:2 * H], in0=s2, scalar=-1.0, in1=extent[:, H:2 * H],
                                               op0=ALU.mult, op1=ALU.max).then_inc(tab_ready, 1)

            def second(b, u):
                if exists(b - 1):
                    take_x1(b - 1, 1 - u)
                if exists(b + 1):
                    rest_a(b + 1, 1 - u)
                if not exists(b - 1):
                    search(1, 1)
                elif isinstance(b, int) and b == 1:
                    dve.wait_ge(whi_ready, 2)
                    nc.vector.tensor_tensor(w_part[1][:], w_raw[:], w_part[0][:].bitcast(F32), ALU.subtract).then_inc(w_ready, 1)
                    nc.vector.tensor_tensor(wo_part[1][:], wo_raw[:], wo_part[0][:].bitcast(F32), ALU.subtract).then_inc(w_ready, 1)
                if exists(b - 1):
                    rest_t(b - 1, 1 - u)
                if exists(b - 1) and exists(b + 1):
                    search(b + 1, 1 - u)
                if exists(b - 1) and exists(b + 1):
                    sum_scores(b - 1, 1 - u)
            pairs(dve, second, peeled=2)
            dve.wait_ge(turned, 2 * NB)
            dve.wait_ge(prod2_done, NB - 1)
            dve.wait_ge(top_kept, NB)
            step = Chain(dve, far_step, 0)
            step(nc.vector.tensor_scalar(top_val[:], top_val[:], -1.0, 1.0, ALU.mult, ALU.add))
            step(nc.vector.tensor_scalar(top_val[:], top_val[:], MASK, None, ALU.mult))
            step(nc.vector.tensor_tensor(far_mask[:], top_val[:], top_val[:, :, 0:1].to_broadcast([P, NB, TOP]), ALU.subtract))
            step(nc.vector.tensor_copy(idx_f[:], top_idx[:]))
            step(nc.vector.tensor_reduce(extent[:, 2 * H:2 * H + 1], far_mask[:, :, TOP - 1], AX.X, ALU.max))
            step(nc.vector.tensor_copy(extent[:, 2 * H + 1:], far_mask[:, :, NARROW]))
            step(nc.vector.memset(scores[0][:], 0.0))
            take_x1(NB - 1, 1)
            sum_scores(NB - 2, 0)
            rest_t(NB - 1, 1)
            dve.wait_ge(seq_copied, NB)
            nc.vector.tensor_tensor(score_products[0][:], table_tile[1][:, 0:D], a1b[:], ALU.mult).then_inc(products_ready, 1)
            sum_scores(NB - 1, 1)

            nc.vector.memset(far[:], 0.0).then_inc(range_ready, 1)
            step = Chain(dve, far_step, 7)
            dve.wait_ge(range_all, 1)
            step(nc.vector.tensor_tensor(ssum[:], extent_all[:, 0:H], extent_all[:, H:2 * H], ALU.add))
            step(nc.vector.tensor_reduce(far[:, 0:1], ssum[:], AX.X, ALU.max))
            step(nc.vector.tensor_scalar(far[:, 1:2], far[:, 0:1], FAR, -1.0, ALU.add, ALU.mult))
            nc.vector.tensor_scalar(flags[:], extent_all[:, 2 * H:], far[:, 1:2], None, ALU.is_ge).then_inc(flags_ready, 1)
            step(nc.vector.tensor_scalar(far_mask[:], far_mask[:], far[:, 1:2], None, ALU.is_lt))
            step(nc.vector.scalar_tensor_tensor(out=slot_idx[:], in0=far_mask[:], scalar=1e6, in1=idx_f[:], op0=ALU.mult, op1=ALU.add))
            nc.vector.tensor_copy(gather_idx[0][:], slot_idx[:, 0, :]).then_inc(near.idx_ready, 1)
            nc.vector.tensor_copy(gather_idx[1][:], slot_idx[:, 1, :]).then_inc(near.idx_ready, 1)
            step(nc.vector.scalar_tensor_tensor(out=top_val[:], in0=far_mask[:], scalar=-1e30, in1=top_val[:], op0=ALU.mult, op1=ALU.add))
            dve.wait_ge(bias_hi_ready, 1)
            nc.vector.tensor_tensor(b_part[1][:], bob[:], b_part[0][:].bitcast(F32), ALU.subtract).then_inc(bias_ready, 1)

            def rest_hidden(path, b, u):
                dve.wait_ge(path.hi_ready, b + 1)
                nc.vector.tensor_tensor(ht_lo[u][:], ps_h[u][:, 0:CT, :], ht_hi[u][:].bitcast(F32), ALU.subtract).then_inc(path.lo_ready, 1)

            def relu(path, b, u):
                if exists(b - 2):
                    dve.wait_ge(path.out_ready, b - 1)
                dve.wait_ge(path.elu_exp, b + 1)
                nc.vector.scalar_tensor_tensor(out=x_tile[u][:], in0=ps_y[:, u, :], scalar=0.0, in1=x1[:, b, :],
                                               op0=ALU.max, op1=ALU.add).then_inc(path.relu_ready, 1)

            def join(path, b, u):
                dve.wait_ge(path.relu_ready, b + 1)
                nc.vector.scalar_tensor_tensor(out=x_tile[u][:], in0=x_norm[u][:], scalar=1.0, in1=x_tile[u][:],
                                               op0=ALU.min, op1=ALU.add).then_inc(path.tail_step, 1)

            def spread(path, b, u):
                dve.wait_ge(path.tail_step, b * 3 + 1)
                nc.vector.bn_stats(stats[:], x_tile[u][:]).then_inc(path.tail_step, 1)

            def moments(path, b, u):
                dve.wait_ge(path.tail_step, b * 3 + 2)
                apart(dve)
                nc.vector.bn_aggr(mean_var[u][:], stats[:]).then_inc(path.tail_step, 1)

            def variance(path, b, u):
                dve.wait_ge(path.tail_step, b * 3 + 3)
                nc.vector.tensor_scalar(var_eps[u][:], mean_var[u][:, 1:2], EPS, None, ALU.add).then_inc(path.var_ready, 1)

            def finish(path, b, u):
                for part in (relu, join, spread, moments, variance):
                    part(path, b, u)

            dve.wait_ge(flags_ready, 1)
            dve.wait_ge(x1_kept, NB)
            dve.wait_ge(small_in, 16 * 3)
            dense = dve.value_load(flags[0:1, 0:1], min_val=0, max_val=1)
            with dve.If(dense == 0):
                def weigh_rows(b, u):
                    wide = dve.value_load(flags[0:1, bass.ds(b + 1, 1)], min_val=0, max_val=1)
                    with dve.If(wide == 0):
                        weigh_slots(b, u, NARROW)
                    with dve.Else():
                        weigh_slots(b, u, SLOTS)

                def weigh_slots(b, u, n):
                    step = Chain(dve, near.weigh_step, b * 7)
                    dve.wait_ge(near.got[u], (b + 2) * (8 * SLOTS) if u == 0 else (b + 1) * (8 * SLOTS))
                    got = rows_got[u][:, 0:n, :]
                    t0, t1, t2 = (t[:, 0:n, :] for t in scores)

                    def over_slots(v):
                        return v.rearrange("p (o h) -> p o h", o=1).to_broadcast([P, n, H])
                    mb = top_val[:, b, 0:n].rearrange("p (k o) -> p k o", o=1).to_broadcast([P, n, H])

                    def beside(part):
                        if exists(b - 3):
                            part(near, b - 3, 1 - u)
                    step.add(nc.vector.tensor_tensor(t0, got[:, :, D:ROW], over_slots(s1[:, b, :]), ALU.add))
                    beside(relu)
                    step.wait()
                    step.add(nc.vector.scalar_tensor_tensor(out=t2, in0=t0, scalar=ALPHA, in1=t0, op0=ALU.mult, op1=ALU.max))
                    beside(join)
                    step.wait()
                    step.add(nc.vector.tensor_tensor(t2, t2, mb, ALU.add))
                    beside(spread)
                    step.wait()
                    step.add(nc.vector.tensor_reduce(smax[:], t2.rearrange("p k h -> p h k"), AX.X, ALU.max))
                    beside(moments)
                    step.wait()
                    nc.vector.tensor_tensor(t0, t2, over_slots(smax[:]), ALU.subtract).then_inc(near.shifted, 1)
                    beside(variance)
                    dve.wait_ge(near.exp_ready, b + 1)
                    step(nc.vector.tensor_reduce(ssum[:], t1.rearrange("p k h -> p h k"), AX.X, ALU.add))
                    step(nc.vector.reciprocal(ssum[:], ssum[:]))
                    step(nc.vector.tensor_tensor(t2, t1, over_slots(ssum[:]), ALU.mult))
                    if exists(b - 2):
                        dve.wait_ge(near.turned, b - 1)
                    nc.vector.tensor_tensor(
                        rows_weighted[u][:, 0:n, :].rearrange("p k (h d) -> p (k h) d", d=DH),
                        got[:, :, 0:D].rearrange("p k (h d) -> p k h d", d=DH),
                        t2.rearrange("p k (h o) -> p k h o", o=1).to_broadcast([P, n, H, DH]), ALU.mult).then_inc(near.weighted, 1)

                def body(b, u):
                    weigh_rows(b, u)
                    if exists(b - 1):
                        rest_hidden(near, b - 1, 1 - u)
                pairs(dve, body, peeled=2)
                finish(near, NB - 3, 1)
                rest_hidden(near, NB - 1, 1)
                finish(near, NB - 2, 0)
                finish(near, NB - 1, 1)
            with dve.Else():
                dve.sem_inc(dense_block, 1)
                with dve.Fori(0, H) as h:
                    dve.wait_ge(head_in, h * 32 + 32)
                    apart(dve)
                    with dve.Fori(0, NB) as b:
                        t = h * NB + b
                        step = Chain(dve, dense_step, t * 6)
                        step(nc.vector.tensor_scalar(dense_score[:], dense_s2[:], s1[:, b, bass.ds(h, 1)], None, ALU.add))
                        step(nc.vector.scalar_tensor_tensor(out=dense_tmp[:], in0=dense_score[:], scalar=ALPHA, in1=dense_score[:],
                                                            op0=ALU.mult, op1=ALU.max))
                        dve.wait_ge(block_in, t * 16 + 16)
                        step(nc.vector.tensor_scalar(stage[0][:], stage[0][:], -1.0, 1.0, ALU.mult, ALU.add))
                        step(nc.vector.scalar_tensor_tensor(out=dense_score[:], in0=stage[0][:], scalar=MASK, in1=dense_tmp[:],
                                                            op0=ALU.mult, op1=ALU.add))
                        step(nc.vector.tensor_reduce(col[:, 0:1], dense_score[:], AX.X, ALU.max))
                        nc.vector.tensor_scalar(col[:, 1:2], col[:, 0:1], -1.0, None, ALU.mult).then_inc(dense_shifted, 1)
                        dve.wait_ge(dense_exp, t + 1)
                        step(nc.vector.reciprocal(col[:, 3:4], col[:, 2:3]))
                        dve.wait_ge(dense_prod, t + 1)
                        nc.vector.tensor_scalar(hidden[:, b, bass.ds(h * DH, DH)], ps_q[:, 0:DH], col[:, 3:4], None,
                                                ALU.mult).then_inc(dense_block, 1)
                dve.wait_ge(dense_block, H * NB + 1)

                def body(b, u):
                    if exists(b - 2):
                        dve.wait_ge(full.turned, b - 1)
                    nc.vector.tensor_copy(rows_weighted[u][:, 0, :], hidden[:, b, :]).then_inc(full.weighted, 1)
                    rest_hidden(full, b, u)
                    if exists(b - 1):
                        finish(full, b - 1, 1 - u)
                pairs(dve, body, peeled=2)
                finish(full, NB - 1, 1)
            dve.nop()

        @block.tensor
        def _(pe):
            pe.wait_ge(consts, 3)
            pe.wait_ge(col_added, NB)
            for k in range(NB):
                mm = nc.tensor.matmul(ps_q[:, k:k + 1], col_partial[:, k * P:(k + 1) * P], ones[:],
                                      start=(k == 0), stop=(k == NB - 1), skip_group_check=True)
            mm.then_inc(col_summed, 1)

            def turn_adj(n, u):
                pe.wait_ge(rows_in[u], n * 8 + 16 - 8 * u)
                if not isinstance(n, int) or n >= 1:
                    if isinstance(n, int) and n > NB:
                        pe.wait_ge(lo_ready, n)
                    elif isinstance(n, int):
                        pe.wait_ge(s_summed, n)
                    else:
                        pe.wait_ge(ps_free[0], n)
                for k in range(NB):
                    mm = nc.tensor.transpose(ps_t[:, k, :], stage[u][:, k * P:(k + 1) * P], ident[:])
                mm.then_inc(turned, 1)

            ps_free = [None]

            def product(b, u, ks, hi, lo, last, done):
                for k in ks:
                    if done is prod1_done and isinstance(b, int) and b == 0:
                        pe.wait_ge(v_ready, k + 1)
                    if done is prod2_done and isinstance(b, int) and b == 0 and k in (0, NB - 1):
                        pe.wait_ge(z_ready, NB - 1 if k == 0 else NB)
                    for n, (m, v) in enumerate(((m_hi, hi), (m_hi, lo), (m_lo, hi))):
                        mm = nc.tensor.matmul(ps_y[:, u, :], m[u][:, k, :], v[:, k, :],
                                              start=(k == 0 and n == 0), stop=(k == NB - 1 and n == 2))
                if last:
                    mm.then_inc(done, 1)

            pe.wait_ge(row_summed, NB)
            turn_adj(0, 0)
            ps_free[0] = s_summed

            def first(b, u):
                turn_adj(b + 1, 1 - u)
                pe.wait_ge(lo_ready, b + 1)
                if exists(b - 2):
                    pe.wait_ge(zt_ready, b - 1)
                product(b, u, range(NB), v_hi, v_lo, True, prod1_done)
            pairs(pe, first)
            ps_free[0] = lo_ready

            def turn_x1(b, u):
                pe.wait_ge(x1_ready, b + 1)
                if exists(b - 1):
                    pe.wait_ge(t_ready, b)
                for c in range(CT):
                    mm = nc.tensor.transpose(ps_x[:, c, :], x_norm[u][:, c * P:(c + 1) * P], ident[:])
                mm.then_inc(x1_turned, 1)

            def project(dst, hi, lo, w, done, bias=()):
                for n, part in enumerate(bias):
                    nc.tensor.matmul(dst, ones_row[0:1, :], part[0:1, :], start=(n == 0), stop=False)
                for c in range(CT):
                    for n, (t, v) in enumerate(((hi, w[0]), (hi, w[1]), (lo, w[0]))):
                        mm = nc.tensor.matmul(dst, t[:, c, :], v[:, c, :], start=(c == 0 and n == 0 and not bias),
                                              stop=(c == CT - 1 and n == 2))
                mm.then_inc(done, 1)

            def features(b):
                pe.wait_ge(t_ready, b + 1)
                if exists(b - 1):
                    pe.wait_ge(seq_copied, b)
                else:
                    pe.wait_ge(w_ready, 2)
                project(ps_q[:], t_hi, t_lo, w_part, seq_done)

            def second(b, u):
                if exists(b + 1):
                    turn_adj(b + (NB + 1), 1 - u)
                pe.wait_ge(lo_ready, b + (NB + 1))
                if exists(b - 2):
                    pe.wait_ge(x1_ready, b - 1)
                else:
                    pe.wait_ge(zt_ready, NB - 1 + b)
                product(b, u, range(0, 6), z_hi, z_lo, False, prod2_done)
                if exists(b - 1):
                    turn_x1(b - 1, 1 - u)
                product(b, u, range(6, 11), z_hi, z_lo, False, prod2_done)
                if exists(b - 1):
                    features(b - 1)
                product(b, u, range(11, NB), z_hi, z_lo, True, prod2_done)
            pairs(pe, second)
            turn_x1(NB - 1, 1)
            features(NB - 1)

            def turn_hidden(path, b, u, slots):
                pe.wait_ge(path.weighted, b + 1)
                if exists(b - 2):
                    pe.wait_ge(path.lo_ready, b - 1)
                for c in range(CT):
                    for k in range(slots):
                        mm = nc.tensor.matmul(ps_h[u][:, c, :], rows_weighted[u][:, k, c * P:(c + 1) * P], ident[:],
                                              start=(k == 0), stop=(k == slots - 1))
                mm.then_inc(path.turned, 1)

            def project_out(path, b, u):
                pe.wait_ge(path.lo_ready, b + 1)
                if exists(b - 2):
                    pe.wait_ge(path.relu_ready, b - 1)
                project(ps_y[:, u, :], ht_hi[u], ht_lo[u], wo_part, path.projected, b_part)

            pe.wait_ge(flags_ready, 1)
            pe.wait_ge(bias_ready, 2)
            dense = pe.value_load(flags[0:1, 0:1], min_val=0, max_val=1)
            with pe.If(dense == 0):
                def step(b, u):
                    wide = pe.value_load(flags[0:1, bass.ds(b + 1, 1)], min_val=0, max_val=1)
                    with pe.If(wide == 0):
                        turn_hidden(near, b, u, NARROW)
                    with pe.Else():
                        turn_hidden(near, b, u, SLOTS)
                    if exists(b - 1):
                        project_out(near, b - 1, 1 - u)
                pairs(pe, step, peeled=2)
                project_out(near, NB - 1, 1)
            with pe.Else():
                with pe.Fori(0, H * NB) as t:
                    pe.wait_ge(dense_exp, t + 1)
                    for k in range(NB):
                        mm = nc.tensor.transpose(ps_t[:, k, :], dense_tmp[:, k * P:(k + 1) * P], ident[:])
                    mm.then_inc(dense_turned, 1)
                    pe.wait_ge(dense_copied, t + 1)
                    for k in range(NB):
                        mm = nc.tensor.matmul(ps_q[:, 0:DH], dense_pT[:, k, :], dense_seq[:, k, :], start=(k == 0), stop=(k == NB - 1))
                    mm.then_inc(dense_prod, 1)

                def step(b, u):
                    turn_hidden(full, b, u, 1)
                    project_out(full, b, u)
                pairs(pe, step, peeled=2)
            pe.nop()


_INS = ['x', 'adj', 'L1_gnn_W_seq', 'L1_gnn_a1', 'L1_gnn_a2', 'L1_gnn_W_out', 'L1_gnn_b_out']
_OUTS = [((2048, 512), 'float32')]


def kernel(**inputs):
    import numpy as _np
    import concourse.bacc as _bacc
    from concourse import mybir as _mybir
    from concourse.bass_utils import run_bass_kernel_spmd as _run

    nc = _bacc.Bacc("TRN2", target_bir_lowering=False, num_devices=1)
    arrays, args = {}, []
    for name in _INS:
        a = _np.ascontiguousarray(inputs[name])
        arrays[f"in_{name}_dram"] = a
        args.append(nc.dram_tensor(f"in_{name}_dram", a.shape, _mybir.dt.from_np(a.dtype), kind="ExternalInput").ap())
    for i, (shape, dtype) in enumerate(_OUTS):
        dt = _mybir.dt.from_np(_np.dtype(dtype))
        args.append(nc.dram_tensor(f"out_{i}_dram", shape, dt, kind="ExternalOutput").ap())
    graph_kernel(nc, *args)
    r = _run(nc, [arrays], core_ids=[0])
    got = tuple(r.results[0][f"out_{i}_dram"] for i in range(len(_OUTS)))
    return got[0]
```
